# Optimizing a Trainium2 kernel written in Bass

```python
import numpy as np
import jax
import jax.numpy as jnp

def _softmax(x, axis=-1):
    return jax.nn.softmax(x, axis=axis)

def _gelu(x):
    return jax.nn.gelu(x, approximate=True)

def _silu(x):
    return jax.nn.silu(x)

def _sigmoid(x):
    return jax.nn.sigmoid(x)

def _layernorm(x, axis=-1, eps=1e-05):
    m = jnp.mean(x, axis=axis, keepdims=True)
    v = jnp.var(x, axis=axis, keepdims=True)
    return (x - m) / jnp.sqrt(v + eps)

def _scatter_add(tgt, idx, src, axis=0):
    return tgt.at[idx].add(src)

def _segment_sum(src, seg, n):
    return jax.ops.segment_sum(src, seg, n)
kernel_name = 'mk_gnn_preln_d2_gnn_r32_ad6626'

def setup_inputs(seed: int=0):
    np.random.seed(seed)
    _w = jnp.asarray

    def _rec_inputs():
        import jax
        import jax.numpy as jnp
        _gk = jax.random.key(seed)
        x = -0.0003713 + 1 * jax.random.normal(jax.random.fold_in(_gk, 1), (3125, 128), jnp.float32)
        src = jax.random.randint(jax.random.fold_in(_gk, 2), (100000,), 0, 3125, jnp.int32)
        dst = jnp.minimum((3125 * jax.random.uniform(jax.random.fold_in(_gk, 3), (100000,)) ** 2.0).astype(jnp.int32), 99999)
        _o = jnp.argsort(dst, stable=True)
        src = src[_o]
        dst = dst[_o]
        edge_type_200 = jax.random.randint(jax.random.fold_in(_gk, 14), (100000,), 0, 200, jnp.int32)
        return (x, src, dst, edge_type_200)
    x, src, dst, edge_type_200 = _rec_inputs()

    def _L0_gnn_setup():
        import jax, jax.numpy as jnp
        import numpy as np
        N_NODES = 3125
        N_EDGES = 20000
        N_RELS = 200
        D = 128
        RRELU_SLOPE = (1.0 / 8.0 + 1.0 / 3.0) / 2.0

        def rrelu(x):
            return jnp.where(x >= 0, x, x * RRELU_SLOPE)

        def _layer(h, e_h, src, dst, iso_mask, norm, W_r, W_sl, W_el):
            self_msg = jnp.where(iso_mask[:, None], h @ W_el, h @ W_sl)
            msg = (e_h + h[src]) @ W_r
            agg = jax.ops.segment_sum(msg, dst, num_segments=h.shape[0])
            return rrelu(agg * norm + self_msg)
        key = jax.random.key(seed)
        ks = jax.random.split(key, 12)
        inp = {'ent_embed': jax.random.normal(ks[0], (N_NODES, D), dtype=jnp.float32), 'rel_embed': jax.random.normal(ks[1], (N_RELS, D), dtype=jnp.float32), 'norm': jax.random.uniform(ks[2], (N_NODES, 1), dtype=jnp.float32), 'src': jax.random.randint(ks[3], (N_EDGES,), 0, N_NODES), 'dst': jax.random.randint(ks[4], (N_EDGES,), 0, N_NODES), 'rel_id': jax.random.randint(ks[5], (N_EDGES,), 0, N_RELS)}
        scale = 1.0 / np.sqrt(D)
        for i, name in enumerate(['W_r1', 'W_sl1', 'W_el1', 'W_r2', 'W_sl2', 'W_el2']):
            inp[name] = jax.random.uniform(ks[6 + i], (D, D), dtype=jnp.float32, minval=-scale, maxval=scale)
        return inp
    _L0_gnn_all = _L0_gnn_setup()
    _L0_gnn_in = {k: v for k, v in _L0_gnn_all.items() if k in ('rel_embed', 'W_r1', 'W_sl1', 'W_el1', 'W_r2', 'W_sl2', 'W_el2')}
    del _L0_gnn_all

    def _L1_gnn_setup():
        import jax, jax.numpy as jnp
        import numpy as np
        import math
        N_NODES = 3125
        N_EDGES = 50000
        DIM = 128
        key = jax.random.key(seed)
        ks = jax.random.split(key, 6)
        x = jax.random.normal(ks[0], (N_NODES, DIM), dtype=jnp.float32)
        edge_index = jax.random.randint(ks[1], (2, N_EDGES), 0, N_NODES, dtype=jnp.int64)
        limit = 0.1 * math.sqrt(6.0 / (DIM + DIM))
        Wqk = jax.random.uniform(ks[2], (DIM, DIM), dtype=jnp.float32, minval=-limit, maxval=limit)
        Wv = jax.random.uniform(ks[3], (DIM, DIM), dtype=jnp.float32, minval=-limit, maxval=limit)
        Wo = jax.random.uniform(ks[4], (DIM, DIM), dtype=jnp.float32, minval=-limit, maxval=limit)
        return {'x': x, 'edge_index': edge_index, 'Wqk': Wqk, 'bqk': jnp.zeros((DIM,), jnp.float32), 'Wv': Wv, 'bv': jnp.zeros((DIM,), jnp.float32), 'Wo': Wo, 'bo': jnp.zeros((DIM,), jnp.float32), 'gamma': jnp.ones((DIM,), jnp.float32), 'beta': jnp.zeros((DIM,), jnp.float32)}
    _L1_gnn_all = _L1_gnn_setup()
    _L1_gnn_in = {k: v for k, v in _L1_gnn_all.items() if k in ('Wqk', 'bqk', 'Wv', 'bv', 'Wo', 'bo', 'gamma', 'beta')}
    del _L1_gnn_all
    return {'x': x, 'src': src, 'dst': dst, 'edge_type_200': edge_type_200, 'L0_gnn_rel_embed': _L0_gnn_in['rel_embed'], 'L0_gnn_W_r1': _L0_gnn_in['W_r1'], 'L0_gnn_W_sl1': _L0_gnn_in['W_sl1'], 'L0_gnn_W_el1': _L0_gnn_in['W_el1'], 'L0_gnn_W_r2': _L0_gnn_in['W_r2'], 'L0_gnn_W_sl2': _L0_gnn_in['W_sl2'], 'L0_gnn_W_el2': _L0_gnn_in['W_el2'], 'L1_gnn_Wqk': _L1_gnn_in['Wqk'], 'L1_gnn_bqk': _L1_gnn_in['bqk'], 'L1_gnn_Wv': _L1_gnn_in['Wv'], 'L1_gnn_bv': _L1_gnn_in['bv'], 'L1_gnn_Wo': _L1_gnn_in['Wo'], 'L1_gnn_bo': _L1_gnn_in['bo'], 'L1_gnn_gamma': _L1_gnn_in['gamma'], 'L1_gnn_beta': _L1_gnn_in['beta']}

def reference(x, src, dst, edge_type_200, L0_gnn_rel_embed, L0_gnn_W_r1, L0_gnn_W_sl1, L0_gnn_W_el1, L0_gnn_W_r2, L0_gnn_W_sl2, L0_gnn_W_el2, L1_gnn_Wqk, L1_gnn_bqk, L1_gnn_Wv, L1_gnn_bv, L1_gnn_Wo, L1_gnn_bo, L1_gnn_gamma, L1_gnn_beta):
    import jax
    import jax.numpy as jnp

    def _L0_gnn_ref(ent_embed, rel_embed, norm, src, dst, rel_id, W_r1, W_sl1, W_el1, W_r2, W_sl2, W_el2):
        import jax, jax.numpy as jnp
        import numpy as np
        N_NODES = 3125
        N_EDGES = 20000
        N_RELS = 200
        D = 128
        RRELU_SLOPE = (1.0 / 8.0 + 1.0 / 3.0) / 2.0

        def rrelu(x):
            return jnp.where(x >= 0, x, x * RRELU_SLOPE)

        def _layer(h, e_h, src, dst, iso_mask, norm, W_r, W_sl, W_el):
            self_msg = jnp.where(iso_mask[:, None], h @ W_el, h @ W_sl)
            msg = (e_h + h[src]) @ W_r
            agg = jax.ops.segment_sum(msg, dst, num_segments=h.shape[0])
            return rrelu(agg * norm + self_msg)
        num_nodes = ent_embed.shape[0]
        e_h = rel_embed[rel_id]
        in_deg = jax.ops.segment_sum(jnp.ones_like(dst), dst, num_segments=num_nodes)
        iso_mask = in_deg == 0
        h = ent_embed
        for W_r, W_sl, W_el in [(W_r1, W_sl1, W_el1), (W_r2, W_sl2, W_el2)]:
            h = _layer(h, e_h, src, dst, iso_mask, norm, W_r, W_sl, W_el)
        return h

    def _L1_gnn_ref(x, edge_index, Wqk, bqk, Wv, bv, Wo, bo, gamma, beta):
        import jax, jax.numpy as jnp
        import numpy as np
        import math
        N_NODES = 3125
        N_EDGES = 50000
        DIM = 128
        N, D = x.shape
        qk = x @ Wqk + bqk
        v = x @ Wv + bv
        src = edge_index[0]
        dst = edge_index[1]
        scores = jnp.sum(qk[dst] * qk[src], axis=-1) / jnp.sqrt(jnp.float32(D))
        scores = jnp.clip(scores, -5.0, 5.0)
        m = jax.ops.segment_max(scores, dst, num_segments=N)
        e = jnp.exp(scores - m[dst])
        s = jax.ops.segment_sum(e, dst, num_segments=N)
        attn = e / s[dst]
        out = jax.ops.segment_sum(attn[:, None] * v[src], dst, num_segments=N)
        out = out @ Wo + bo
        h = out + x
        mu = jnp.mean(h, axis=-1, keepdims=True)
        var = jnp.mean(jnp.square(h - mu), axis=-1, keepdims=True)
        return gamma * (h - mu) / jnp.sqrt(var + 1e-05) + beta
    edge_index = jnp.stack([src, dst])
    deg = jnp.maximum(jax.ops.segment_sum(jnp.ones(dst.shape, jnp.float32), dst, num_segments=3125), 1.0)
    deg_isqrt = deg ** (-0.5)
    h = jnp.maximum(_layernorm(x, axis=-1), 0.0)
    x = x + _L0_gnn_ref(h, L0_gnn_rel_embed, deg_isqrt[:, None], src, dst, edge_type_200, L0_gnn_W_r1, L0_gnn_W_sl1, L0_gnn_W_el1, L0_gnn_W_r2, L0_gnn_W_sl2, L0_gnn_W_el2)
    h = jnp.maximum(_layernorm(x, axis=-1), 0.0)
    x = x + _L1_gnn_ref(h, edge_index, L1_gnn_Wqk, L1_gnn_bqk, L1_gnn_Wv, L1_gnn_bv, L1_gnn_Wo, L1_gnn_bo, L1_gnn_gamma, L1_gnn_beta)
    return x

_drawn_inputs = setup_inputs


def setup_inputs(seed=0):
    import zlib

    import numpy as np

    out = dict(_drawn_inputs(seed))
    spreads = {'L1_gnn_bqk': (0.0, 2.0),
     'L1_gnn_bv': (0.0, 0.8),
     'L1_gnn_bo': (0.0, 0.276),
     'L1_gnn_gamma': (1.0, 0.2),
     'L1_gnn_beta': (0.0, 0.1)}
    factors = {'L1_gnn_Wqk': 8.0, 'L1_gnn_Wv': 8.0, 'L1_gnn_Wo': 8.0}
    for name, (base, spread) in spreads.items():
        noise = np.random.default_rng([zlib.crc32(name.encode()), seed]).standard_normal(out[name].shape)
        drawn = base * np.exp(spread * noise) if base else spread * noise
        out[name] = jnp.asarray(drawn.astype(out[name].dtype))
    for name, factor in factors.items():
        out[name] = (out[name] * factor).astype(out[name].dtype)
    return out
```

```python
from contextlib import ExitStack

import numpy as np
import concourse.bass as bass
from concourse import mybir

F32 = mybir.dt.float32
F16 = mybir.dt.float16
BF16 = mybir.dt.bfloat16
I32 = mybir.dt.int32
ALU = mybir.AluOpType
ACT = mybir.ActivationFunctionType
AX = mybir.AxisListType

N = 3125
E = 100000
D = 128
RELS = 200
NP = 125
NB = N // NP
TILES = E // NP
RH = 2
RL = RELS // RH
PL = NB + RH
GT = 4
GROUPS = TILES // GT
BT = 8
BATCHES = TILES // BT
W = 12
WG = 39
HA = 13
HBK = NB - HA
ER = 100
EB = TILES // ER
EPS = 1e-5
SLOPE = (1.0 / 8.0 + 1.0 / 3.0) / 2.0
WORK = 42976
ROUND = 1.5 * 2.0**23


def view(base, at, rows, cols, dt):
    size = {F32: 4, I32: 4, F16: 2, BF16: 2}[dt]
    v = base[0:rows, at // 4:(at + cols * size) // 4]
    return v if dt == F32 else v.bitcast(dt)


def build_counts(nc, ctx, T, src, dst, rel, x, parts_dram):
    counts, work = T["counts"], T["work"]

    def sem(name):
        return ctx.enter_context(nc.semaphore(name))

    local = ExitStack()

    def ps(name, shape, dt=F32):
        return local.enter_context(nc.psum_tensor(name, shape, dt))

    lo_b = BT * 2 * D * 2
    m_b = BT * NB * W * 2
    r_b = BT * RH * WG * 2
    ring = []
    at = 0
    for i in range(2):
        ring.append((
            view(work, at, NP, BT * 2 * D, F16).rearrange("p (t k c) -> p t k c", t=BT, k=2),
            view(work, at + lo_b, NP, BT * NB * W, F16).rearrange("p (t c) -> p t c", t=BT),
            view(work, at + lo_b + m_b, NP, BT * RH * WG, F16).rearrange("p (t c) -> p t c", t=BT)))
        at += lo_b + m_b + r_b
    key_lo = view(work, at, NP, TILES * 4, F16).rearrange("p (t k) -> p t k", k=4)
    at += TILES * 8
    key_m = view(work, at, NP, TILES * 2, F16).rearrange("p (t k) -> p t k", k=2)
    at += TILES * 4
    key_r = view(work, at, NP, TILES * 2, F16).rearrange("p (t k) -> p t k", k=2)
    at += TILES * 4
    iota_h = view(work, at, NP, 2 * NP * 0 + NB * W, F16)
    at += NB * W * 2
    places = view(work, at, 1, (GROUPS + 1) * (1 + GT), I32).rearrange("p (g k) -> p g k", k=1 + GT)
    at += (GROUPS + 1) * (1 + GT) * 4
    ones = view(work, at, ER, NP, F32)
    at += NP * 4
    iota_f = view(work, at, 128, NB * W, I32)
    at += NB * W * 4
    x_in = view(work, at, NP, D, F32)
    at += 4 * D
    tmp = view(work, at, NP, D, F32)
    at += 4 * D
    split = view(work, at, NP, 3 * D, BF16).rearrange("p (s f) -> p s f", s=3)
    at += 6 * D
    stat = view(work, at, NP, 8, F32)
    one_over, eps, power, zero = (stat[:, k:k + 1] for k in range(4, 8))
    at += 32
    assert at <= WORK

    PZ = 20
    flat = T["counts_flat"][:, PZ * N:PL * N + PL * N % 2]
    at = 0

    def scratch(rows, cols, dt):
        nonlocal at
        size = 4
        v = flat[0:rows, at // 2:(at + cols * size) // 2].bitcast(dt)
        at += cols * size
        return v

    edges_i = scratch(ER, 3 * EB * NP, I32).rearrange("p (a b c) -> p a b c", a=3, b=EB)
    edges_f = scratch(ER, 3 * EB * NP, F32).rearrange("p (a b c) -> p a b c", a=3, b=EB)
    hi, t1, loc, dlt, val = (scratch(NP, TILES, F32) for _ in range(5))
    diag = view(work, 0, ER, EB * ER, F32).rearrange("p (b c) -> p b c", b=EB)
    first = view(work, 4 * EB * ER, ER, EB, F32)
    base = view(work, 4 * EB * ER + 64, NP, GROUPS, F32)
    rh = view(work, 4 * EB * ER + 64 + 4 * GROUPS, NP, TILES, F32)
    ident, ident_h = T["ident"], T["ident_h"]

    pe_src, pe_dst, pe_rel, pe_min = (ps(n, [128, 2, 512]) for n in ("pe_src", "pe_dst", "pe_rel", "pe_min"))
    half = EB // 2 * ER
    of = lambda p: p[0:NP, :, 0:half]
    two = lambda v: v.rearrange("p (a b) -> p a b", a=2)

    edges_in = [sem(f"edges_in{i}") for i in range(3)]
    consts = sem("consts")
    iota_done = sem("iota_done")
    as_float = sem("as_float")
    diag_done = sem("diag_done")
    turned = sem("turned")
    keys_done = sem("keys_done")
    cleared = sem("cleared")
    cleared_pool = sem("cleared_pool")
    prep = sem("prep")
    norm_step, norm_mid, x_loaded, parts_out = sem("norm_step"), sem("norm_mid"), sem("x_loaded"), sem("parts_out")
    ring_ready = sem("ring_ready")
    ring_free = sem("ring_free")
    sum_a, sum_b, sum_r = sem("sum_a"), sem("sum_b"), sem("sum_r")
    put_a, put_b, put_r = sem("put_a"), sem("put_b"), sem("put_r")

    with nc.Block() as block:

        @block.sync
        def _(sp):
            for a, v in enumerate((dst, src, rel)):
                sp.dma_start(edges_i[:, a, :, :], v.rearrange("(b p c) -> p b c", p=ER, c=NP)).then_inc(edges_in[a], 16)

        @block.gpsimd
        def _(pool):
            pool.memset(ident[:, :], 0.0).then_inc(consts, 1)
            pool.memset(ident_h[:, :], 0.0).then_inc(consts, 1)
            pool.iota(iota_f, pattern=[[1, NB * W]], base=0, channel_multiplier=0).then_inc(iota_done, 1)
            pool.memset(ones[:, :], 1.0).then_inc(consts, 1)
            pool.wait_ge(consts, 3)
            for m in (ident, ident_h):
                pool.affine_select(out=m[:, :], in_=m[:, :], compare_op=ALU.not_equal, fill=1.0, base=0,
                                   pattern=[[-1, 128]], channel_multiplier=1).then_inc(consts, 1)
            pool.memset(T["counts_flat"][:, 0:PZ * N].bitcast(F32), 0.0).then_inc(cleared_pool, 1)

        @block.tensor
        def _(pe):
            pe.wait_ge(consts, 5)
            for a, out in enumerate((pe_dst, pe_src, pe_rel)):
                pe.wait_ge(as_float, a + 1)
                for b in range(EB):
                    k, c = divmod(b, EB // 2)
                    last = pe.transpose(out[0:NP, k, c * ER:(c + 1) * ER], edges_f[:, a, b, :], ident[0:ER, 0:ER])
                last.then_inc(turned, 1)
            pe.wait_ge(diag_done, 1)
            for b in range(EB):
                k, c = divmod(b, EB // 2)
                last = pe.matmul(pe_min[0:NP, k, c * ER:(c + 1) * ER], ones[:, :], diag[:, b, :], start=True, stop=True)
            last.then_inc(turned, 1)

        @block.vector
        def _(dve):
            steps = [0]

            def link(ins):
                steps[0] += 1
                ins.then_inc(prep, 1)
                dve.wait_ge(prep, steps[0])

            for a in range(3):
                dve.wait_ge(edges_in[a], 16)
                dve.tensor_copy(edges_f[:, a, :, :], edges_i[:, a, :, :]).then_inc(as_float, 1)
                if a == 0:
                    dve.wait_ge(as_float, 1)
                    link(dve.tensor_reduce(first, edges_f[:, 0, :, :], AX.X, ALU.min))
                    dve.wait_ge(consts, 5)
                    dve.tensor_tensor(diag, ident[0:ER, None, 0:ER].broadcast_to([ER, EB, ER]),
                                      first[:, :, None].broadcast_to([ER, EB, ER]), ALU.mult).then_inc(diag_done, 1)
            dve.wait_ge(iota_done, 1)
            dve.tensor_copy(iota_h, iota_f[0:NP, :])
            dup = lambda v: v[:, :, None].broadcast_to([NP, TILES, 2])
            dve.wait_ge(turned, 2)
            link(dve.tensor_scalar(two(t1), of(pe_src), float(-(NP // 2)), 1.0 / NP, ALU.add, ALU.mult))
            link(dve.tensor_scalar(hi, t1, ROUND, -ROUND, ALU.add, ALU.add))
            link(dve.scalar_tensor_tensor(two(t1), two(hi), float(-NP), of(pe_src), ALU.mult, ALU.add))
            link(dve.tensor_copy(key_lo[:, :, 0:2], dup(t1)))
            dve.wait_ge(turned, 3)
            link(dve.tensor_scalar(two(rh), of(pe_rel), float(RL), None, ALU.is_ge))
            link(dve.scalar_tensor_tensor(two(t1), two(rh), float(-RL), of(pe_rel), ALU.mult, ALU.add))
            link(dve.tensor_copy(key_lo[:, :, 2:4], dup(t1)))
            dve.wait_ge(turned, 4)
            link(dve.tensor_copy(two(t1), of(pe_min)))
            link(dve.tensor_reduce(base, t1.rearrange("p (g t) -> p g t", t=GT), AX.X, ALU.min))
            link(dve.tensor_scalar(base, base, float(N - WG), None, ALU.min))
            base_t = base[:, :, None].broadcast_to([NP, GROUPS, GT])
            grp = lambda v: v.rearrange("p (g t) -> p g t", t=GT)
            link(dve.tensor_tensor(grp(dlt), grp(t1), base_t, ALU.subtract))
            link(dve.tensor_scalar(dlt, dlt, float(WG - W), None, ALU.min))
            link(dve.tensor_tensor(grp(t1), grp(dlt), base_t, ALU.add))
            link(dve.tensor_tensor(two(loc), of(pe_dst), two(t1), ALU.subtract))
            link(dve.tensor_copy(places[:, 1:, 0:1], base[0:1, :, None]))
            link(dve.tensor_copy(places[:, 1:, 1:], grp(dlt[0:1, :])))
            link(dve.tensor_scalar(val, loc, 0.0, None, ALU.is_ge))
            link(dve.scalar_tensor_tensor(val, loc, float(W - 1), val, ALU.is_le, ALU.mult))
            for h, key, w in ((hi, key_m, W), (rh, key_r, WG)):
                if w == WG:
                    link(dve.tensor_tensor(loc, loc, dlt, ALU.add))
                link(dve.scalar_tensor_tensor(t1, h, float(w), loc, ALU.mult, ALU.add))
                link(dve.scalar_tensor_tensor(t1, t1, 1.0, val, ALU.add, ALU.mult))
                link(dve.tensor_scalar(key, dup(t1), -1.0, None, ALU.add))
            dve.memset(flat.bitcast(F32), 0.0).then_inc(cleared, 1)
            dve.wait_ge(cleared, 1)

    for p in (local,):
        p.close()
    banks = [[ps(f"group{i}{n}", [128, 512]) for n in "abr"] for i in range(2)]

    with nc.Block() as block:

        @block.vector
        def _(dve):
            with dve.Fori(0, BATCHES // 2) as it:
                for hb in range(2):
                    lo, m, r = ring[hb]
                    dve.wait_ge(ring_free, it * 2 + (hb + 1))
                    t0 = (it * 2 + hb) * BT
                    kl = key_lo[:, bass.ds(t0, BT), :].rearrange("p t (k two) -> p (t k) two", two=2)
                    dve.tensor_tensor(lo.rearrange("p t k (c two) -> p (t k) c two", two=2),
                                      iota_h[:, None, 0:D].rearrange("p o (c two) -> p o c two", two=2).broadcast_to([NP, 2 * BT, D // 2, 2]),
                                      kl[:, :, None, :].broadcast_to([NP, 2 * BT, D // 2, 2]), ALU.is_equal)
                    last = None
                    for out, key, n in ((m, key_m, NB * W), (r, key_r, RH * WG)):
                        last = dve.tensor_tensor(out.rearrange("p t (c two) -> p t c two", two=2),
                                                 iota_h[:, None, 0:n].rearrange("p o (c two) -> p o c two", two=2).broadcast_to([NP, BT, n // 2, 2]),
                                                 key[:, bass.ds(t0, BT), None, :].broadcast_to([NP, BT, n // 2, 2]), ALU.is_equal)
                    last.then_inc(ring_ready, 1)

        @block.gpsimd
        def _(pool):
            pool.memset(one_over, 1.0 / D).then_inc(put_a, 1)
            pool.memset(eps, EPS).then_inc(put_b, 1)
            pool.memset(power, -0.5).then_inc(put_r, 1)
            pool.memset(zero, 0.0).then_inc(ring_free, 2)
            with pool.Fori(0, NB) as j:
                steps = [0]

                def link(ins):
                    steps[0] += 1
                    ins.then_inc(norm_step, 1)
                    pool.wait_ge(norm_step, j * 24 + steps[0])

                def total(out, v):
                    link(pool.tensor_tensor(tmp[:, 0:D // 2], v[:, 0:D // 2], v[:, D // 2:D], ALU.add))
                    n = D // 4
                    while n > 1:
                        link(pool.tensor_tensor(tmp[:, 0:n], tmp[:, 0:n], tmp[:, n:2 * n], ALU.add))
                        n //= 2
                    link(pool.tensor_tensor(out, tmp[:, 0:1], tmp[:, 1:2], ALU.add))

                pool.dma_start(x_in, x[bass.ds(j * NP, NP), :]).then_inc(x_loaded, 16)
                pool.wait_ge(x_loaded, j * 16 + 16)
                def over(v):
                    return v.broadcast_to([NP, D])

                total(stat[:, 0:1], x_in)
                link(pool.tensor_tensor(stat[:, 0:1], stat[:, 0:1], one_over, ALU.mult))
                link(pool.tensor_tensor(x_in, x_in, over(stat[:, 0:1]), ALU.subtract))
                link(pool.tensor_tensor(tmp, x_in, x_in, ALU.mult))
                total(stat[:, 1:2], tmp)
                ins = pool.tensor_tensor(stat[:, 1:2], stat[:, 1:2], one_over, ALU.mult)
                pool.tensor_scalar(x_in, x_in, 0.0, None, ALU.max).then_inc(norm_mid, 1)
                link(ins)
                link(pool.tensor_tensor(stat[:, 1:2], stat[:, 1:2], eps, ALU.add))
                link(pool.tensor_tensor(stat[:, 2:3], stat[:, 1:2], power, ALU.pow))
                pool.wait_ge(norm_mid, j * 2 + 1)
                link(pool.tensor_tensor(x_in, x_in, over(stat[:, 2:3]), ALU.mult))
                link(pool.tensor_tensor(split[:, 0, :], x_in, over(zero), ALU.add))
                link(pool.tensor_tensor(x_in, x_in, split[:, 0, :], ALU.subtract))
                link(pool.tensor_tensor(split[:, 1, :], x_in, over(zero), ALU.add))
                pool.tensor_tensor(split[:, 2, :], x_in, split[:, 1, :], ALU.subtract).then_inc(norm_mid, 1)
                pool.wait_ge(norm_mid, j * 2 + 2)
                pool.dma_start(parts_dram[bass.ds(j * NP, NP), :], split.rearrange("p s f -> p (s f)")).then_inc(parts_out, 16)
                pool.wait_ge(parts_out, j * 16 + 16)

        @block.tensor
        def _(pe):
            regs = [[pe.alloc_register(f"place{g}_{k}") for k in range(1 + GT)] for g in range(4)]
            with pe.Fori(0, BATCHES // 2) as it:
                for hb in range(2):
                    lo, m, r = ring[hb]
                    pe.wait_ge(ring_ready, it * 2 + (hb + 1))
                    for g in range(2):
                        a, b, c = banks[g]
                        win = [a[:, 0:HA * WG].rearrange("p (h d) -> p h d", d=WG),
                               b[:, 0:HBK * WG].rearrange("p (h d) -> p h d", d=WG),
                               c[:, 0:RH * WG].rearrange("p (h d) -> p h d", d=WG)]
                        grp = it * 4 + (hb * 2 + g + 1)
                        pe.reg_load(regs[hb * 2 + g], places[0:1, bass.ds(grp, 1), :])
                        at0 = pe.snap(regs[hb * 2 + g][0], donate=True, min_val=0, max_val=N - WG)
                        shift = [pe.snap(x, donate=True, min_val=0, max_val=WG - W) for x in regs[hb * 2 + g][1:]]
                        for t in range(GT):
                            k = g * GT + t
                            d0 = shift[t]
                            s = t == 0
                            pe.matmul(win[0][:, :, bass.ds(d0, W)], lo[:, k, 0, :],
                                      m[:, k, 0:HA * W].rearrange("p (h d) -> p h d", d=W), start=s, stop=False, skip_group_check=True)
                            pe.matmul(win[1][:, :, bass.ds(d0, W)], lo[:, k, 0, :],
                                      m[:, k, HA * W:].rearrange("p (h d) -> p h d", d=W), start=s, stop=False, skip_group_check=True)
                            last = pe.matmul(c[:, 0:RH * WG], lo[:, k, 1, :], r[:, k, :], start=s, stop=False)
                        if g:
                            last.then_inc(ring_free, 1)
                        for w, put, done, h0, h1 in ((win[0], put_a, sum_a, 0, HA), (win[1], put_b, sum_b, HA, NB), (win[2], put_r, sum_r, NB, PL)):
                            pe.wait_ge(put, grp)
                            pe.matmul(w, ident_h[:, :], counts[:, h0:h1, bass.ds(at0, WG)], start=False, stop=True,
                                      skip_group_check=w is not win[2]).then_inc(done, 1)

        @block.scalar
        def _(act):
            regs = [act.alloc_register(f"start{g}") for g in range(8)]
            with act.Fori(0, GROUPS // 8) as it:
                for g in range(8):
                    act.reg_load(regs[g], places[0:1, bass.ds(it * 8 + (g + 1), 1), 0:1])
                    at0 = act.snap(regs[g], donate=True, min_val=0, max_val=N - WG)
                    for p, n, put, done, h0, h1 in ((banks[g % 2][0], HA, put_a, sum_a, 0, HA), (banks[g % 2][1], HBK, put_b, sum_b, HA, NB),
                                                    (banks[g % 2][2], RH, put_r, sum_r, NB, PL)):
                        act.wait_ge(done, it * 8 + (g + 1))
                        act.copy(counts[:, h0:h1, bass.ds(at0, WG)],
                                 p[:, 0:n * WG].rearrange("p (h d) -> p h d", d=WG)).then_inc(put, 1)
    local.close()


LB = 2
PARTS_B = NB * 3 * D * 2
HN_B = NB * D * 4


def message_layer(nc, ctx, T, layer, w_r, w_sl, w_el, aux):
    counts, work, small, ident, ident_h = T["counts"], T["work"], T["small"], T["ident"], T["ident_h"]
    last_layer = layer == 2
    L = f"l{layer}_"

    def sem(name):
        return ctx.enter_context(nc.semaphore(L + name))

    at = 0

    def place(rows, cols, dt, size):
        nonlocal at
        v = view(work, at, rows, cols, dt)
        at += cols * size
        assert at <= WORK
        return v

    parts = place(NP, NB * 3 * D, BF16, 2).rearrange("p (j s f) -> p j s f", s=3, f=D)
    hn = place(128, NB * D, F32, 4)
    hn_n = hn[0:NP, :].rearrange("p (j f) -> p j f", f=D)
    rel_parts = place(RL, RH * 3 * D, BF16, 2).rearrange("p (h s f) -> p h s f", s=3, f=D)
    wr = place(D, D, F32, 4)
    ws = place(D, 2 * D, F32, 4)
    agg_t = place(D, LB * NP, F32, 4)
    h_t = place(D, LB * NP, F32, 4)
    tmp = place(NP, LB * D, F32, 4).rearrange("p (b f) -> p b f", f=D)
    if last_layer:
        wqk = place(D, D, F32, 4)
        xc = place(NP, LB * D, F32, 4).rearrange("p (b f) -> p b f", f=D)
        h3_t = place(D, LB * NP, F32, 4)
        bqk = place(D, 1, F32, 4)
        bn = place(NP, LB * 6, F32, 4).rearrange("p (b k) -> p b k", k=6)
        mv = place(NP, LB * 2, F32, 4).rearrange("p (b k) -> p b k", k=2)
        rstd = place(NP, LB, F32, 4)
        mark = place(1, 1, F32, 4)
        qk_t = hn
    else:
        rel_f = place(RL, RH * D, F32, 4).rearrange("p (h f) -> p h f", f=D)
        ones_h = place(RL, 2, F16, 2)[:, 0:1]
    norm, iso, some = small[:, 0, :], small[:, 1, :], small[:, 2, :]

    local = ExitStack()

    def ps(name, shape):
        return local.enter_context(nc.psum_tensor(L + name, shape, F32))

    ps_h, ps_g, ps_s, ps_a = ps("ps_h", [128, 512]), ps("ps_g", [128, 512]), ps("ps_s", [128, 512]), ps("ps_a", [128, 512])
    ps_x, ps_q = ps("ps_x", [128, 512]), ps("ps_q", [128, 512])
    self_v = ps_s[0:NP, :].rearrange("p (b k f) -> p b k f", b=LB, k=2)
    agg_v = ps_a[0:NP, 0:LB * D].rearrange("p (b f) -> p b f", f=D)

    wts, parts_in = sem("weights_in"), [sem(f"parts_in{i}") for i in range(5)]
    rel_step, parts_ready, deg_done, deg_step = sem("rel_step"), sem("parts_ready"), sem("deg_done"), sem("deg_step")
    ones_set = sem("ones_set")
    turned, turned_out, summed, summed_out = sem("turned"), sem("turned_out"), sem("summed"), sem("summed_out")
    self_done, agg_done, el_out, step, chunk_done = sem("self_done"), sem("agg_done"), sem("el_out"), sem("step"), sem("chunk_done")
    x_in, x2_ready, x2_out, h3_ready, h3_out = sem("x_in"), sem("x2_ready"), sem("x2_out"), sem("h3_ready"), sem("h3_out")
    var_done, sq_done, h3_turned, h3_t_out, qk_done, qk_out = (sem(n) for n in ("var_done", "sq_done", "h3_turned", "h3_t_out", "qk_done", "qk_out"))
    FULL = NB // LB

    with nc.Block() as block:

        @block.sync
        def _(sp):
            if not last_layer:
                for i in range(5):
                    sp.dma_start(parts[:, 5 * i:5 * i + 5, :, :],
                                 aux["parts"].rearrange("(j p) (s f) -> p j s f", p=NP, s=3)[:, 5 * i:5 * i + 5, :, :]).then_inc(parts_in[i], 16)
                sp.dma_start(rel_f, aux["rel"].rearrange("(h p) f -> p h f", p=RL)).then_inc(wts, 16)
            sp.dma_start(wr, w_r).then_inc(wts, 16)
            sp.dma_start(ws[:, 0:D], w_sl).then_inc(wts, 16)
            sp.dma_start(ws[:, D:], w_el).then_inc(wts, 16)
            if last_layer:
                sp.dma_start(wqk, aux["wqk"]).then_inc(wts, 16)
                sp.dma_start(bqk, aux["bqk"].rearrange("(p o) -> p o", o=1)).then_inc(wts, 16)

                def chunk(c, nb):
                    known = isinstance(c, int)
                    at, before, this = (v if known else sp.snap(v) for v in (c * (LB * NP), c * 16, c + 1))
                    rows = lambda v: v[bass.ds(at, nb * NP), :].rearrange("(b p) f -> p b f", p=NP)
                    if not known or c > 0:
                        sp.wait_ge(h3_out, before)
                        sp.wait_ge(h3_turned, c)
                    sp.dma_start(xc[:, 0:nb, :], rows(aux["x"])).then_inc(x_in, 16)
                    sp.wait_ge(x2_ready, this)
                    sp.dma_start(rows(aux["x2"]), tmp[:, 0:nb, :]).then_inc(x2_out, 16)
                    sp.wait_ge(h3_ready, this)
                    sp.dma_start(rows(aux["h3"]), xc[:, 0:nb, :]).then_inc(h3_out, 16)

                chunk(0, LB)
                with sp.Fori(1, FULL) as c:
                    chunk(c, LB)
                chunk(FULL, NB - FULL * LB)
                sp.wait_ge(x2_out, 16 * (FULL + 1))
                sp.wait_ge(h3_out, 16 * (FULL + 1))

        @block.tensor
        def _(pe):
            if not last_layer:
                pe.wait_ge(ones_set, 1)
                for j in range(NB):
                    for h in range(RH):
                        last = pe.matmul(ps_x[0:NP, j:j + 1], counts[0:RL, NB + h, j * NP:(j + 1) * NP], ones_h, start=h == 0, stop=h == RH - 1)
                last.then_inc(deg_done, 1)

            def own(c, nb):
                for b in range(nb):
                    for s in range(3):
                        if isinstance(c, int):
                            lhs = parts[:, c * LB + b, s, :]
                        else:
                            lhs = parts[:, bass.ds(c * LB + b, 1), s, :].rearrange("p o f -> p (o f)")
                        last = pe.matmul(ps_h[:, b * NP:(b + 1) * NP], lhs, ident_h[0:NP, 0:NP], start=s == 0, stop=s == 2)
                last.then_inc(turned, 1)

            def sums(c, nb, first=False):
                cols = bass.ds(c * (LB * NP), nb * NP)
                for j in range(NB):
                    if first and j % 5 == 0:
                        (pe.wait_ge(parts_ready, 2 * (j // 5) + 2) if last_layer else pe.wait_ge(parts_in[j // 5], 16))
                    for s in range(3):
                        pe.matmul(ps_g[:, 0:nb * NP], parts[:, j, s, :], counts[0:NP, j, cols], start=j == 0 and s == 0, stop=False)
                if first and not last_layer:
                    pe.wait_ge(rel_step, 6)
                for h in range(RH):
                    for s in range(3):
                        last = pe.matmul(ps_g[:, 0:nb * NP], rel_parts[:, h, s, :], counts[0:RL, NB + h, cols], start=False, stop=h == RH - 1 and s == 2)
                last.then_inc(summed, 1)

            def h3_turn(c, nb):
                pe.wait_ge(h3_ready, c + 1)
                for b in range(nb):
                    last = pe.transpose(ps_x[:, b * NP:(b + 1) * NP], xc[:, b, :], ident[0:NP, 0:NP])
                last.then_inc(h3_turned, 1)

            def weigh(c, nb, first=False):
                if first:
                    pe.wait_ge(wts, 16 * (5 if last_layer else 4))
                pe.wait_ge(turned_out, c + 1)
                if not first:
                    pe.wait_ge(chunk_done, c)
                for b in range(nb):
                    last = pe.matmul(self_v[:, b, :, :].rearrange("p k f -> p (k f)"), h_t[:, b * NP:(b + 1) * NP], ws, start=True, stop=True)
                last.then_inc(self_done, 1)
                pe.wait_ge(summed_out, c + 1)
                for b in range(nb):
                    last = pe.matmul(agg_v[:, b, :], agg_t[:, b * NP:(b + 1) * NP], wr, start=True, stop=True)
                last.then_inc(agg_done, 1)

            def qk(c, nb):
                pe.wait_ge(h3_t_out, c + 1)
                pe.matmul(ps_q[:, 0:nb * NP], wqk, h3_t[:, 0:nb * NP], start=True, stop=True).then_inc(qk_done, 1)

            if last_layer:
                pe.wait_ge(parts_ready, 2)
            else:
                pe.wait_ge(parts_in[0], 16)
            own(0, LB)
            sums(0, LB, True)
            weigh(0, LB, True)
            with pe.Fori(1, FULL) as c:
                own(c, LB)
                sums(c, LB)
                if last_layer:
                    h3_turn(c - 1, LB)
                weigh(c, LB)
                if last_layer:
                    qk(c - 1, LB)
            own(FULL, NB - FULL * LB)
            sums(FULL, NB - FULL * LB)
            if last_layer:
                h3_turn(FULL - 1, LB)
            weigh(FULL, NB - FULL * LB)
            if last_layer:
                qk(FULL - 1, LB)
                h3_turn(FULL, NB - FULL * LB)
                qk(FULL, NB - FULL * LB)

        @block.scalar
        def _(act):
            if last_layer:
                for i in range(5):
                    v = slice(5 * i, 5 * i + 5)
                    act.copy(parts[:, v, 0, :], hn_n[:, v, :]).then_inc(rel_step, 1)
                    act.wait_ge(parts_ready, 2 * i + 1)
                    act.copy(parts[:, v, 1, :], hn_n[:, v, :]).then_inc(rel_step, 1)
            else:
                act.wait_ge(deg_step, 3)
                act.activation(norm, norm, ACT.Sqrt).then_inc(deg_step, 1)

            def chunk(c, nb):
                act.wait_ge(turned, c + 1)
                act.copy(h_t[:, 0:nb * NP], ps_h[:, 0:nb * NP]).then_inc(turned_out, 1)
                act.wait_ge(summed, c + 1)
                act.copy(agg_t[:, 0:nb * NP], ps_g[:, 0:nb * NP]).then_inc(summed_out, 1)
                if last_layer and not (isinstance(c, int) and c == 0):
                    late(c - 1, LB)
                act.wait_ge(self_done, c + 1)
                for b in range(nb):
                    at = (c * LB + b)
                    act.mul(tmp[:, b, :], self_v[:, b, 1, :], iso[:, bass.ds(at, 1)]).then_inc(el_out, 1)
                if last_layer:
                    act.wait_ge(var_done, c + 1)
                    act.activation(rstd[:, 0:nb], mv[:, 0:nb, 1], ACT.Sqrt).then_inc(sq_done, 1)

            def late(c, nb):
                act.wait_ge(h3_turned, c + 1)
                act.copy(h3_t[:, 0:nb * NP], ps_x[:, 0:nb * NP]).then_inc(h3_t_out, 1)

            def rows(c, nb):
                act.wait_ge(qk_done, c + 1)
                act.activation(qk_t[:, bass.ds(c * (LB * NP), nb * NP)], ps_q[:, 0:nb * NP], ACT.Identity, bias=bqk).then_inc(qk_out, 1)

            if last_layer:
                act.wait_ge(wts, 16 * 5)
            chunk(0, LB)
            with act.Fori(1, FULL) as c:
                chunk(c, LB)
                if last_layer:
                    rows(c - 1, LB)
            chunk(FULL, NB - FULL * LB)
            if last_layer:
                rows(FULL - 1, LB)
                late(FULL, NB - FULL * LB)
                rows(FULL, NB - FULL * LB)

        @block.vector
        def _(dve):
            if last_layer:
                for i in range(5):
                    v = slice(5 * i, 5 * i + 5)
                    dve.wait_ge(rel_step, 2 * i + 1)
                    dve.tensor_tensor(hn_n[:, v, :], hn_n[:, v, :], parts[:, v, 0, :], ALU.subtract).then_inc(parts_ready, 1)
                    dve.wait_ge(rel_step, 2 * i + 2)
                    dve.tensor_tensor(parts[:, v, 2, :], hn_n[:, v, :], parts[:, v, 1, :], ALU.subtract).then_inc(parts_ready, 1)
            else:
                dve.memset(ones_h, 1.0).then_inc(ones_set, 1)
                dve.wait_ge(deg_done, 1)
                dve.tensor_scalar(iso, ps_x[0:NP, 0:NB], 0.0, None, ALU.is_equal).then_inc(deg_step, 1)
                dve.tensor_scalar(some, ps_x[0:NP, 0:NB], 0.0, None, ALU.is_gt).then_inc(deg_step, 1)
                dve.tensor_scalar(norm, ps_x[0:NP, 0:NB], 1.0, None, ALU.max).then_inc(deg_step, 1)
                dve.wait_ge(deg_step, 4)
                dve.reciprocal(norm, norm).then_inc(deg_step, 1)
                dve.wait_ge(deg_step, 5)
                dve.wait_ge(wts, 16 * 4)
                for s in range(3):
                    dve.tensor_copy(rel_parts[:, :, s, :], rel_f).then_inc(rel_step, 1)
                    dve.wait_ge(rel_step, 2 * s + 1)
                    dve.tensor_tensor(rel_f, rel_f, rel_parts[:, :, s, :], ALU.subtract).then_inc(rel_step, 1)
                    dve.wait_ge(rel_step, 2 * s + 2)

            def chunk(c, nb, per):
                done = [0]

                def link(ins):
                    done[0] += 1
                    ins.then_inc(step, 1)
                    dve.wait_ge(step, c * per + done[0])

                dve.wait_ge(el_out, c * LB + nb)
                for b in range(nb):
                    dve.scalar_tensor_tensor(tmp[:, b, :], self_v[:, b, 0, :], some[:, bass.ds(c * LB + b, 1)], tmp[:, b, :], ALU.mult, ALU.add)\
                       .then_inc(step, 1)
                    done[0] += 1
                dve.wait_ge(agg_done, c + 1)
                dve.wait_ge(step, c * per + done[0])
                for b in range(nb):
                    ins = dve.scalar_tensor_tensor(tmp[:, b, :], agg_v[:, b, :], norm[:, bass.ds(c * LB + b, 1)], tmp[:, b, :], ALU.mult, ALU.add)
                    done[0] += 1
                    ins.then_inc(step, 1)
                dve.wait_ge(step, c * per + done[0])
                t = tmp[:, 0:nb, :]
                if not last_layer:
                    dve.scalar_tensor_tensor(hn_n[:, bass.ds(c * LB, nb), :], t, SLOPE, t, ALU.mult, ALU.max).then_inc(chunk_done, 1)
                    return
                xv = xc[:, 0:nb, :]
                link(dve.scalar_tensor_tensor(t, t, SLOPE, t, ALU.mult, ALU.max))
                dve.wait_ge(x_in, c * 16 + 16)
                dve.tensor_tensor(t, t, xv, ALU.add).then_inc(x2_ready, 1)
                dve.wait_ge(x2_ready, c + 1)
                for b in range(nb):
                    ins = dve.bn_stats(bn[:, b, :], tmp[:, b, :])
                    done[0] += 1
                    ins.then_inc(step, 1)
                dve.wait_ge(step, c * per + done[0])
                dve.tensor_copy(mark, bn[0:1, 0, 0:1])
                for b in range(nb):
                    ins = dve.bn_aggr(mv[:, b, :], bn[:, b, :])
                    done[0] += 1
                    ins.then_inc(step, 1)
                dve.wait_ge(step, c * per + done[0])
                dve.tensor_scalar(mv[:, 0:nb, 1], mv[:, 0:nb, 1], EPS, None, ALU.add).then_inc(var_done, 1)
                dve.wait_ge(sq_done, c + 1)
                link(dve.reciprocal(rstd[:, 0:nb], rstd[:, 0:nb]))
                for b in range(nb):
                    link(dve.tensor_scalar(xc[:, b, :], tmp[:, b, :], mv[:, b, 0:1], rstd[:, b:b + 1], ALU.subtract, ALU.mult))
                dve.tensor_scalar(xv, xv, 0.0, None, ALU.max).then_inc(h3_ready, 1)
                dve.wait_ge(x2_out, c * 16 + 16)
                dve.memset(rstd[0:1, 0:1], 1.0).then_inc(chunk_done, 1)

            per = 2 * LB + (2 + 3 * LB if last_layer else 0)
            chunk(0, LB, per)
            with dve.Fori(1, FULL) as c:
                chunk(c, LB, per)
            chunk(FULL, NB - FULL * LB, per)
    local.close()


AB = 4
CLIP = 5.0


def attention(nc, ctx, T, wv, bv, wo, bo, gamma, beta, x2, h3d, out):
    counts, work, small = T["counts"], T["work"], T["small"]

    def sem(name):
        return ctx.enter_context(nc.semaphore("a_" + name))

    at = 0

    def place(rows, cols):
        nonlocal at
        v = view(work, at, rows, cols, F32)
        at += cols * 4
        assert at <= WORK
        return v

    WIDE = AB * NP
    h3 = place(NP, NB * D).rearrange("p (j f) -> p j f", f=D)
    pbuf = [place(NP, WIDE) for _ in range(3)]
    ones, zero = place(NP, 1), place(NP, 1)
    bv_c = place(D, 1)
    inv = place(NP, AB)
    bn = place(NP, 2 * 6).rearrange("p (b k) -> p b k", k=6)
    mv = place(NP, 2 * 2).rearrange("p (b k) -> p b k", k=2)
    rstd = place(NP, 2)
    mark = place(1, 1)
    assert at <= PARTS_B
    at = PARTS_B
    qk_t = place(D, N)
    acc = place(NP, WIDE)
    hv = place(D, WIDE)
    y = place(NP, 2 * D).rearrange("p (b f) -> p b f", f=D)
    xr = place(NP, 2 * D).rearrange("p (b f) -> p b f", f=D)
    bo_b, gamma_b, beta_b, bvo = (place(NP, D) for _ in range(4))
    wv_s, wo_s = place(D, D), place(D, D)
    some = small[:, 2, :]

    local = ExitStack()

    def ps(name):
        return local.enter_context(nc.psum_tensor("a_" + name, [128, 512], F32))

    ps_s = [ps(f"ps_s{i}") for i in range(4)]
    ps_o, ps_v, ps_f, ps_n = ps("ps_o"), ps("ps_v"), ps("ps_f"), ps("ps_n")
    scores, clipped, exped, p_ready, pv_done, acc_done = (sem(n) for n in ("scores", "clipped", "exped", "p_ready", "pv_done", "acc_done"))
    loaded, h3_in, ones_set, bvb, bvo_done, bvo_out = (sem(n) for n in ("loaded", "h3_in", "ones_set", "bvb", "bvo_done", "bvo_out"))
    n_done, hv_out, v_done, v_out, f_done, inv_step, step = (sem(n) for n in ("n_done", "hv_out", "v_done", "v_out", "f_done", "inv_step", "step"))
    zero_set = sem("zero_set")
    var_done, sq_done, xr_in, y_ready, y_out = (sem(n) for n in ("var_done", "sq_done", "xr_in", "y_ready", "y_out"))
    FULL = NB // AB

    def bc(v):
        return v.rearrange("(o f) -> o f", o=1).broadcast_to([NP, D])

    def pairs(nb):
        return [(h, min(2, nb - 2 * h)) for h in range((nb + 1) // 2)]

    with nc.Block() as block:

        @block.sync
        def _(sp):
            sp.dma_start(h3, h3d.rearrange("(j p) f -> p j f", p=NP)).then_inc(h3_in, 16)
            for s, v in ((wv_s, wv), (wo_s, wo), (bv_c, bv.rearrange("(p o) -> p o", o=1)), (bo_b, bc(bo)), (gamma_b, bc(gamma)), (beta_b, bc(beta))):
                sp.dma_start(s, v).then_inc(loaded, 16)

            def ends(c, nb):
                for h, n in pairs(nb):
                    known = isinstance(c, int)
                    at, q, this = (v if known else sp.snap(v) for v in (c * WIDE + 2 * h * NP, c * 2 + h, c * 2 + (h + 1)))
                    rows = lambda v: v[bass.ds(at, n * NP), :].rearrange("(b p) f -> p b f", p=NP)
                    if not (known and q == 0):
                        sp.wait_ge(y_ready, q)
                    sp.dma_start(xr[:, 0:n, :], rows(x2)).then_inc(xr_in, 16)
                    sp.wait_ge(y_ready, this)
                    sp.dma_start(rows(out), y[:, 0:n, :]).then_inc(y_out, 16)

            ends(0, AB)
            with sp.Fori(1, FULL) as c:
                ends(c, AB)
            ends(FULL, NB - FULL * AB)
            sp.wait_ge(y_out, 16 * (2 * FULL + 1))

        @block.tensor
        def _(pe):
            def score(c, nb, j):
                last = pe.matmul(ps_s[j % 4][0:NP, 0:nb * NP], qk_t[:, j * NP:(j + 1) * NP], qk_t[:, bass.ds(c * WIDE, nb * NP)],
                                 start=True, stop=True)
                last.then_inc(scores, 1)

            def chunk(c, nb, prev):
                for j in range(3):
                    score(c, nb, j)
                if prev:
                    pe.wait_ge(acc_done, c * NB)
                    for b in range(prev):
                        last = pe.matmul(ps_n[0:NP, b:b + 1], acc[:, b * NP:(b + 1) * NP], ones, start=True, stop=True)
                    last.then_inc(n_done, 1)
                    pe.wait_ge(hv_out, c)
                for j in range(NB):
                    if j + 3 < NB:
                        score(c, nb, j + 3)
                    pe.wait_ge(p_ready, c * NB + (j + 1))
                    pe.matmul(ps_o[:, 0:nb * NP], h3[:, j, :], pbuf[j % 3][:, 0:nb * NP], start=j == 0, stop=j == NB - 1).then_inc(pv_done, 1)
                    if prev and j == 2:
                        project(c - 1, prev)
                    if prev and j == 5:
                        final(c - 1, prev)

            def project(c, nb):
                pe.wait_ge(hv_out, c + 1)
                pe.matmul(ps_v[:, 0:nb * NP], wv_s, hv[:, 0:nb * NP], start=True, stop=True).then_inc(v_done, 1)

            def final(c, nb):
                pe.wait_ge(v_out, c + 1)
                for b in range(nb):
                    last = pe.matmul(ps_f[0:NP, b * D:(b + 1) * D], hv[:, b * NP:(b + 1) * NP], wo_s, start=True, stop=True)
                last.then_inc(f_done, 1)

            pe.wait_ge(bvb, 1)
            pe.matmul(ps_f[0:NP, 0:D], hv[:, 0:NP], wo_s, start=True, stop=True).then_inc(bvo_done, 1)
            pe.wait_ge(h3_in, 16)
            pe.wait_ge(ones_set, 1)
            chunk(0, AB, 0)
            with pe.Fori(1, FULL) as c:
                chunk(c, AB, AB)
            rest = NB - FULL * AB
            chunk(FULL, rest, AB)
            pe.wait_ge(acc_done, (FULL + 1) * NB)
            for b in range(rest):
                last = pe.matmul(ps_n[0:NP, b:b + 1], acc[:, b * NP:(b + 1) * NP], ones, start=True, stop=True)
            last.then_inc(n_done, 1)
            project(FULL, rest)
            final(FULL, rest)

        @block.gpsimd
        def _(pool):
            def chunk(c, nb):
                for j in range(NB):
                    pool.wait_ge(p_ready, c * NB + (j + 1))
                    p = pbuf[j % 3][:, 0:nb * NP]
                    a = acc[:, 0:nb * NP]
                    if j == 0:
                        if not isinstance(c, int) or c > 0:
                            pool.wait_ge(n_done, c)
                        pool.tensor_tensor(a, p, zero.broadcast_to([NP, nb * NP]), ALU.add).then_inc(acc_done, 1)
                    else:
                        pool.wait_ge(acc_done, c * NB + j)
                        pool.tensor_tensor(a, a, p, ALU.add).then_inc(acc_done, 1)

            pool.memset(zero, 0.0).then_inc(zero_set, 1)
            pool.wait_ge(zero_set, 1)
            chunk(0, AB)
            with pool.Fori(1, FULL) as c:
                chunk(c, AB)
            chunk(FULL, NB - FULL * AB)

        @block.scalar
        def _(act):
            def take(c, nb):
                act.wait_ge(pv_done, (c + 1) * NB)
                act.copy(hv[:, 0:nb * NP], ps_o[:, 0:nb * NP]).then_inc(hv_out, 1)

            def projected(c, nb):
                act.wait_ge(v_done, c + 1)
                act.copy(hv[:, 0:nb * NP], ps_v[:, 0:nb * NP]).then_inc(v_out, 1)

            def root(c, h, n):
                act.wait_ge(var_done, c * 2 + (h + 1))
                act.activation(rstd[:, 0:n], mv[:, 0:n, 1], ACT.Sqrt).then_inc(sq_done, 1)

            def chunk(c, nb, prev):
                for j in range(NB):
                    act.wait_ge(clipped, c * NB + (j + 1))
                    s = ps_s[j % 4][0:NP, 0:nb * NP]
                    act.activation(s, s, ACT.Exp, scale=float(D) ** -0.5).then_inc(exped, 1)
                    if prev:
                        if j == 0:
                            take(c - 1, prev)
                        if j == 4:
                            projected(c - 1, prev)
                        for h, n in pairs(prev):
                            if j == 10 + 7 * h:
                                root(c - 1, h, n)

            act.wait_ge(bvo_done, 1)
            act.copy(bvo, ps_f[0:NP, 0:D]).then_inc(bvo_out, 1)
            chunk(0, AB, 0)
            with act.Fori(1, FULL) as c:
                chunk(c, AB, AB)
            rest = NB - FULL * AB
            chunk(FULL, rest, AB)
            take(FULL, rest)
            projected(FULL, rest)
            for h, n in pairs(rest):
                root(FULL, h, n)

        @block.vector
        def _(dve):
            PER = 2 + 2 + 1 + 2 + 2 + 1 + 2 + 1 + 1

            def clip(c, nb, j):
                dve.wait_ge(scores, c * NB + (j + 1))
                s = ps_s[j % 4][0:NP, 0:nb * NP]
                dve.tensor_scalar(s, s, CLIP * float(D) ** 0.5, -CLIP * float(D) ** 0.5, ALU.min, ALU.max).then_inc(clipped, 1)

            def weigh(c, nb, j):
                dve.wait_ge(exped, c * NB + (j + 1))
                if not (isinstance(c, int) and c == 0 and j < 3):
                    dve.wait_ge(pv_done, c * NB + (j - 2 if j else 0))
                    dve.wait_ge(acc_done, c * NB + (j - 2 if j else 0))
                dve.tensor_tensor(pbuf[j % 3][:, 0:nb * NP], ps_s[j % 4][0:NP, 0:nb * NP], counts[0:NP, j, bass.ds(c * WIDE, nb * NP)],
                                  ALU.mult).then_inc(p_ready, 1)

            def begin(c, nb):
                dve.wait_ge(n_done, c + 1)
                dve.tensor_scalar(inv[:, 0:nb], ps_n[0:NP, 0:nb], 1e-30, None, ALU.max).then_inc(inv_step, 1)
                dve.wait_ge(inv_step, c * 2 + 1)
                dve.reciprocal(inv[:, 0:nb], inv[:, 0:nb]).then_inc(inv_step, 1)
                dve.wait_ge(inv_step, c * 2 + 2)
                dve.wait_ge(f_done, c + 1)

            def counted(c, h):
                done = [0]

                def tick(ins):
                    done[0] += 1
                    ins.then_inc(step, 1)

                def join():
                    dve.wait_ge(step, (c * 2 + h) * PER + done[0])

                return done, tick, join

            def stats(c, h, n):
                done, tick, join = counted(c, h)
                if not (isinstance(c, int) and c == 0 and h == 0):
                    dve.wait_ge(y_out, (c * 2 + h) * 16)
                at = c * AB + 2 * h
                for b in range(n):
                    tick(dve.scalar_tensor_tensor(y[:, b, :], ps_f[0:NP, (2 * h + b) * D:(2 * h + b + 1) * D], inv[:, 2 * h + b:2 * h + b + 1],
                                                  h3[:, bass.ds(at + b, 1), :].rearrange("p o f -> p (o f)"), ALU.mult, ALU.add))
                join()
                for b in range(n):
                    tick(dve.scalar_tensor_tensor(y[:, b, :], bvo, some[:, bass.ds(at + b, 1)], y[:, b, :], ALU.mult, ALU.add))
                join()
                tick(dve.tensor_tensor(y[:, 0:n, :], y[:, 0:n, :], bo_b[:, None, :].broadcast_to([NP, n, D]), ALU.add))
                join()
                for b in range(n):
                    tick(dve.bn_stats(bn[:, b, :], y[:, b, :]))
                join()
                dve.tensor_copy(mark, bn[0:1, 0, 0:1])
                for b in range(n):
                    tick(dve.bn_aggr(mv[:, b, :], bn[:, b, :]))
                join()
                dve.tensor_scalar(mv[:, 0:n, 1], mv[:, 0:n, 1], EPS, None, ALU.add).then_inc(var_done, 1)
                return done[0]

            def finish(c, h, n, base):
                done, tick, join = counted(c, h)
                done[0] = base
                dve.wait_ge(sq_done, c * 2 + (h + 1))
                tick(dve.reciprocal(rstd[:, 0:n], rstd[:, 0:n]))
                join()
                for b in range(n):
                    tick(dve.tensor_scalar(y[:, b, :], y[:, b, :], mv[:, b, 0:1], rstd[:, b:b + 1], ALU.subtract, ALU.mult))
                join()
                tick(dve.tensor_tensor(y[:, 0:n, :], y[:, 0:n, :], gamma_b[:, None, :].broadcast_to([NP, n, D]), ALU.mult))
                join()
                tick(dve.tensor_tensor(y[:, 0:n, :], y[:, 0:n, :], beta_b[:, None, :].broadcast_to([NP, n, D]), ALU.add))
                join()
                dve.wait_ge(xr_in, (c * 2 + h) * 16 + 16)
                dve.tensor_tensor(y[:, 0:n, :], y[:, 0:n, :], xr[:, 0:n, :], ALU.add).then_inc(y_ready, 1)

            def chunk(c, nb, prev):
                clip(c, nb, 0)
                clip(c, nb, 1)
                base = 0
                for j in range(NB):
                    if j + 2 < NB:
                        clip(c, nb, j + 2)
                    weigh(c, nb, j)
                    if prev:
                        for h, n in pairs(prev):
                            if j == 9 + 7 * h:
                                if h == 0:
                                    begin(c - 1, prev)
                                base = stats(c - 1, h, n)
                            if j == 12 + 7 * h:
                                finish(c - 1, h, n, base)

            dve.memset(ones, 1.0).then_inc(ones_set, 1)
            dve.wait_ge(loaded, 16 * 6)
            dve.tensor_copy(hv[:, 0:NP], bv_c.broadcast_to([D, NP])).then_inc(bvb, 1)
            dve.wait_ge(bvo_out, 1)
            chunk(0, AB, 0)
            with dve.Fori(1, FULL) as c:
                chunk(c, AB, AB)
            rest = NB - FULL * AB
            chunk(FULL, rest, AB)
            for h, n in pairs(rest):
                if h == 0:
                    begin(FULL, rest)
                finish(FULL, h, n, stats(FULL, h, n))
    local.close()


def program(nc, x, src, dst, rel, rel_embed, w_r1, w_sl1, w_el1, w_r2, w_sl2, w_el2, wqk, bqk, wv, bv, wo, bo, gamma, beta, out):
    parts_dram = nc.dram_tensor("h_parts", (N, 3 * D), BF16).ap()
    x2 = nc.dram_tensor("x_after_messages", (N, D), F32).ap()
    h3 = nc.dram_tensor("h_attention", (N, D), F32).ap()
    with ExitStack() as ctx:
        def sb(name, shape, dt):
            return ctx.enter_context(nc.sbuf_tensor(name, shape, dt))

        flat = sb("counts", [128, PL * N + PL * N % 2], F16)
        T = {"counts_flat": flat, "counts": flat[:, 0:PL * N].rearrange("p (h d) -> p h d", d=N),
             "work": sb("work", [128, WORK // 4], F32), "ident": sb("ident", [128, 128], F32),
             "ident_h": sb("ident_h", [128, 128], F16), "small": sb("small", [NP, 3, NB], F32)}
        build_counts(nc, ctx, T, src, dst, rel, x, parts_dram)
        message_layer(nc, ctx, T, 1, w_r1, w_sl1, w_el1, {"parts": parts_dram, "rel": rel_embed})
        message_layer(nc, ctx, T, 2, w_r2, w_sl2, w_el2, {"x": x, "x2": x2, "h3": h3, "wqk": wqk, "bqk": bqk})
        attention(nc, ctx, T, wv, bv, wo, bo, gamma, beta, x2, h3, out)


_INS = ["x", "src", "dst", "edge_type_200", "L0_gnn_rel_embed", "L0_gnn_W_r1", "L0_gnn_W_sl1", "L0_gnn_W_el1", "L0_gnn_W_r2", "L0_gnn_W_sl2",
        "L0_gnn_W_el2", "L1_gnn_Wqk", "L1_gnn_bqk", "L1_gnn_Wv", "L1_gnn_bv", "L1_gnn_Wo", "L1_gnn_bo", "L1_gnn_gamma", "L1_gnn_beta"]


def kernel(**inputs):
    import concourse.bacc as bacc
    from concourse.bass_utils import run_bass_kernel_spmd

    nc = bacc.Bacc("TRN2", target_bir_lowering=False, num_devices=1)
    arrays, args = {}, []
    for name in _INS:
        a = np.ascontiguousarray(inputs[name])
        arrays[f"in_{name}"] = a
        args.append(nc.dram_tensor(f"in_{name}", a.shape, mybir.dt.from_np(a.dtype), kind="ExternalInput").ap())
    args.append(nc.dram_tensor("out_0", (N, D), F32, kind="ExternalOutput").ap())
    program(nc, *args)
    r = run_bass_kernel_spmd(nc, [arrays], core_ids=[0])
    return r.results[0]["out_0"]
```

```python
from contextlib import ExitStack

import numpy as np
import concourse.bass as bass
from concourse import mybir

F32 = mybir.dt.float32
F16 = mybir.dt.float16
BF16 = mybir.dt.bfloat16
I32 = mybir.dt.int32
ALU = mybir.AluOpType
ACT = mybir.ActivationFunctionType
AX = mybir.AxisListType

N = 3125
E = 100000
D = 128
RELS = 200
NP = 125
NB = N // NP
TILES = E // NP
RH = 2
RL = RELS // RH
PL = NB + RH
GT = 4
GROUPS = TILES // GT
BT = 8
BATCHES = TILES // BT
W = 12
WG = 36
HA = 14
HBK = NB - HA
ER = 100
EB = TILES // ER
EPS = 1e-5
SLOPE = (1.0 / 8.0 + 1.0 / 3.0) / 2.0
WORK = 42880
ROUND = 1.5 * 2.0**23


def view(base, at, rows, cols, dt):
    size = {F32: 4, I32: 4, F16: 2, BF16: 2}[dt]
    v = base[0:rows, at // 4:(at + cols * size) // 4]
    return v if dt == F32 else v.bitcast(dt)


def build_counts(nc, ctx, T, src, dst, rel, x, parts_dram):
    counts, work = T["counts"], T["work"]

    def sem(name):
        return ctx.enter_context(nc.semaphore(name))

    local = ExitStack()

    def ps(name, shape, dt=F32):
        return local.enter_context(nc.psum_tensor(name, shape, dt))

    lo_b = BT * 2 * D * 2
    m_b = BT * NB * W * 2
    r_b = BT * RH * WG * 2
    ring = []
    at = 0
    for i in range(2):
        ring.append((
            view(work, at, NP, BT * 2 * D, F16).rearrange("p (t k c) -> p t k c", t=BT, k=2),
            view(work, at + lo_b, NP, BT * NB * W, F16).rearrange("p (t c) -> p t c", t=BT),
            view(work, at + lo_b + m_b, NP, BT * RH * WG, F16).rearrange("p (t c) -> p t c", t=BT)))
        at += lo_b + m_b + r_b
    key_lo = view(work, at, NP, TILES * 4, F16).rearrange("p (t k) -> p t k", k=4)
    at += TILES * 8
    key_m = view(work, at, NP, TILES * 2, F16).rearrange("p (t k) -> p t k", k=2)
    at += TILES * 4
    key_r = view(work, at, NP, TILES * 2, F16).rearrange("p (t k) -> p t k", k=2)
    at += TILES * 4
    iota_h = view(work, at, NP, NB * W, F16)
    at += NB * W * 2
    places = view(work, at, 1, (GROUPS + 1) * (1 + GT), I32).rearrange("p (g k) -> p g k", k=1 + GT)
    at += (GROUPS + 1) * (1 + GT) * 4
    table = view(work, at, 1, 1, F32)
    one_row = view(work, at + 4, 1, 1, F32)
    at += 8
    ones = view(work, at, ER, NP, F32)
    at += NP * 4
    iota_f = view(work, at, 128, NB * W, I32)
    at += NB * W * 4
    x_in = view(work, at, NP, D, F32)
    at += 4 * D
    xc = view(work, at, NP, D, F32)
    at += 4 * D
    tmp = view(work, at, NP, D, F32)
    at += 4 * D
    split = view(work, at, NP, 3 * D, BF16).rearrange("p (s f) -> p s f", s=3)
    at += 6 * D
    stat = view(work, at, NP, 8, F32)
    one_over, eps, power, zero = (stat[:, k:k + 1] for k in range(4, 8))
    at += 32
    assert at <= WORK

    PZ = 20
    flat = T["counts_flat"][:, PZ * N:PL * N + PL * N % 2]
    SPLIT = (PL - PZ) * N // 4 * 2
    at = 0

    def scratch(rows, cols, dt):
        nonlocal at
        size = 4
        v = flat[0:rows, at // 2:(at + cols * size) // 2].bitcast(dt)
        at += cols * size
        return v

    edges_i = scratch(ER, 3 * EB * NP, I32).rearrange("p (a b c) -> p a b c", a=3, b=EB)
    edges_f = scratch(ER, 3 * EB * NP, F32).rearrange("p (a b c) -> p a b c", a=3, b=EB)
    hi, t1, loc, dlt, val = (scratch(NP, TILES, F32) for _ in range(5))
    diag = view(work, 0, ER, EB * ER, F32).rearrange("p (b c) -> p b c", b=EB)
    first = view(work, 4 * EB * ER, ER, EB, F32)
    base = view(work, 4 * EB * ER + 64, NP, GROUPS, F32)
    rh = view(work, 4 * EB * ER + 64 + 4 * GROUPS, NP, TILES, F32)
    ident, ident_h = T["ident"], T["ident_h"]

    pe_src, pe_dst, pe_rel, pe_min = (ps(n, [128, 2, 512]) for n in ("pe_src", "pe_dst", "pe_rel", "pe_min"))
    half = EB // 2 * ER
    of = lambda p: p[0:NP, :, 0:half]
    two = lambda v: v.rearrange("p (a b) -> p a b", a=2)

    edges_in = [sem(f"edges_in{i}") for i in range(3)]
    consts = sem("consts")
    iota_done = sem("iota_done")
    as_float = sem("as_float")
    diag_done = sem("diag_done")
    turned = sem("turned")
    keys_done = sem("keys_done")
    cleared = sem("cleared")
    cleared_pool = sem("cleared_pool")
    prep = sem("prep")
    norm_step, norm_mid, x_loaded, x_free, parts_out = (sem(n) for n in ("norm_step", "norm_mid", "x_loaded", "x_free", "parts_out"))
    ring_ready = sem("ring_ready")
    ring_free = sem("ring_free")
    table_in = sem("table_in")
    sum_a, sum_b = sem("sum_a"), sem("sum_b")
    put_a, put_b = sem("put_a"), sem("put_b")
    powers = sem("powers")

    with nc.Block() as block:

        @block.sync
        def _(sp):
            for a, v in enumerate((dst, src, rel)):
                sp.dma_start(edges_i[:, a, :, :], v.rearrange("(b p c) -> p b c", p=ER, c=NP)).then_inc(edges_in[a], 16)

        @block.gpsimd
        def _(pool):
            pool.memset(ident[:, :], 0.0).then_inc(consts, 1)
            pool.memset(one_row, 1.0).then_inc(table_in, 1)
            pool.memset(ident_h[:, :], 0.0).then_inc(consts, 1)
            pool.iota(iota_f, pattern=[[1, NB * W]], base=0, channel_multiplier=0).then_inc(iota_done, 1)
            pool.memset(ones[:, :], 1.0).then_inc(consts, 1)
            pool.wait_ge(consts, 3)
            for m in (ident, ident_h):
                pool.affine_select(out=m[:, :], in_=m[:, :], compare_op=ALU.not_equal, fill=1.0, base=0,
                                   pattern=[[-1, 128]], channel_multiplier=1).then_inc(consts, 1)
            pool.memset(T["counts_flat"][:, 0:PZ * N].bitcast(F32), 0.0).then_inc(cleared_pool, 1)
            pool.wait_ge(keys_done, 2)
            pool.memset(flat[:, SPLIT:].bitcast(F32), 0.0).then_inc(cleared_pool, 1)
            pool.wait_ge(cleared_pool, 2)

        @block.tensor
        def _(pe):
            pe.wait_ge(consts, 5)
            for a, out in enumerate((pe_dst, pe_src, pe_rel)):
                pe.wait_ge(as_float, a + 1)
                for b in range(EB):
                    k, c = divmod(b, EB // 2)
                    last = pe.transpose(out[0:NP, k, c * ER:(c + 1) * ER], edges_f[:, a, b, :], ident[0:ER, 0:ER])
                last.then_inc(turned, 1)
            pe.wait_ge(diag_done, 1)
            for b in range(EB):
                k, c = divmod(b, EB // 2)
                last = pe.matmul(pe_min[0:NP, k, c * ER:(c + 1) * ER], ones[:, :], diag[:, b, :], start=True, stop=True)
            last.then_inc(turned, 1)

        @block.vector
        def _(dve):
            steps = [0]

            def link(ins):
                steps[0] += 1
                ins.then_inc(prep, 1)
                dve.wait_ge(prep, steps[0])

            for a in range(3):
                dve.wait_ge(edges_in[a], 16)
                dve.tensor_copy(edges_f[:, a, :, :], edges_i[:, a, :, :]).then_inc(as_float, 1)
                if a == 0:
                    dve.wait_ge(as_float, 1)
                    link(dve.tensor_reduce(first, edges_f[:, 0, :, :], AX.X, ALU.min))
                    dve.wait_ge(consts, 5)
                    dve.tensor_tensor(diag, ident[0:ER, None, 0:ER].broadcast_to([ER, EB, ER]),
                                      first[:, :, None].broadcast_to([ER, EB, ER]), ALU.mult).then_inc(diag_done, 1)
            dve.wait_ge(iota_done, 1)
            dve.tensor_copy(iota_h, iota_f[0:NP, :])
            dup = lambda v: v[:, :, None].broadcast_to([NP, TILES, 2])
            dve.wait_ge(turned, 2)
            link(dve.tensor_scalar(two(t1), of(pe_src), float(-(NP // 2)), 1.0 / NP, ALU.add, ALU.mult))
            link(dve.tensor_scalar(hi, t1, ROUND, -ROUND, ALU.add, ALU.add))
            link(dve.scalar_tensor_tensor(two(t1), two(hi), float(-NP), of(pe_src), ALU.mult, ALU.add))
            link(dve.tensor_copy(key_lo[:, :, 0:2], dup(t1)))
            dve.wait_ge(turned, 3)
            link(dve.tensor_scalar(two(rh), of(pe_rel), float(RL), None, ALU.is_ge))
            link(dve.scalar_tensor_tensor(two(t1), two(rh), float(-RL), of(pe_rel), ALU.mult, ALU.add))
            link(dve.tensor_copy(key_lo[:, :, 2:4], dup(t1)))
            dve.wait_ge(turned, 4)
            link(dve.tensor_copy(two(t1), of(pe_min)))
            link(dve.tensor_reduce(base, t1.rearrange("p (g t) -> p g t", t=GT), AX.X, ALU.min))
            link(dve.tensor_scalar(base, base, float(N - WG), None, ALU.min))
            base_t = base[:, :, None].broadcast_to([NP, GROUPS, GT])
            grp = lambda v: v.rearrange("p (g t) -> p g t", t=GT)
            link(dve.tensor_tensor(grp(dlt), grp(t1), base_t, ALU.subtract))
            link(dve.tensor_scalar(dlt, dlt, float(WG - W), None, ALU.min))
            link(dve.tensor_tensor(grp(t1), grp(dlt), base_t, ALU.add))
            link(dve.tensor_tensor(two(loc), of(pe_dst), two(t1), ALU.subtract))
            link(dve.tensor_copy(places[:, 1:, 0:1], base[0:1, :, None]))
            link(dve.tensor_copy(places[:, 1:, 1:], grp(dlt[0:1, :])))
            link(dve.tensor_scalar(val, loc, 0.0, None, ALU.is_ge))
            link(dve.scalar_tensor_tensor(val, loc, float(W - 1), val, ALU.is_le, ALU.mult))
            link(dve.tensor_reduce(T["outside"][:, :], val, AX.X, ALU.add))
            link(dve.tensor_scalar(T["outside"][:, :], T["outside"][:, :], -1.0, float(TILES), ALU.mult, ALU.add))
            for h, key, w in ((hi, key_m, W), (rh, key_r, WG)):
                if w == WG:
                    link(dve.tensor_tensor(loc, loc, dlt, ALU.add))
                link(dve.scalar_tensor_tensor(t1, h, float(w), loc, ALU.mult, ALU.add))
                link(dve.scalar_tensor_tensor(t1, t1, 1.0, val, ALU.add, ALU.mult))
                ins = dve.tensor_scalar(key, dup(t1), -1.0, None, ALU.add)
                ins.then_inc(keys_done, 1)
                dve.wait_ge(keys_done, 1 if key is key_m else 2)
            dve.memset(flat[:, 0:SPLIT].bitcast(F32), 0.0).then_inc(cleared, 1)
            dve.wait_ge(cleared, 1)

    for p in (local,):
        p.close()
    banks = [[ps(f"group{i}{n}", [128, 512]) for n in "ab"] for i in range(2)]

    with nc.Block() as block:

        @block.sync
        def _(sp):
            def load(j):
                sp.dma_start(x_in, x[bass.ds(j * NP, NP), :]).then_inc(x_loaded, 16)

            def store(j):
                sp.dma_start(parts_dram[bass.ds(j * NP, NP), :], split.rearrange("p s f -> p (s f)")).then_inc(parts_out, 16)

            load(0)
            with sp.Fori(0, NB - 1) as j:
                at_in, at_out, turn = sp.snap((j + 1) * NP), sp.snap(j * NP), sp.snap(j * 2 + 2)
                sp.wait_ge(x_free, j + 1)
                sp.dma_start(x_in, x[bass.ds(at_in, NP), :]).then_inc(x_loaded, 16)
                sp.wait_ge(norm_mid, turn)
                sp.dma_start(parts_dram[bass.ds(at_out, NP), :], split.rearrange("p s f -> p (s f)")).then_inc(parts_out, 16)
            sp.wait_ge(norm_mid, 2 * NB)
            store(NB - 1)
            sp.wait_ge(parts_out, 16 * (NB + 1))

        @block.vector
        def _(dve):
            with dve.Fori(0, BATCHES // 2) as it:
                for hb in range(2):
                    lo, m, r = ring[hb]
                    dve.wait_ge(ring_free, it * 2 + (hb + 1))
                    t0 = (it * 2 + hb) * BT
                    kl = key_lo[:, bass.ds(t0, BT), :].rearrange("p t (k two) -> p (t k) two", two=2)
                    dve.tensor_tensor(lo.rearrange("p t k (c two) -> p (t k) c two", two=2),
                                      iota_h[:, None, 0:D].rearrange("p o (c two) -> p o c two", two=2).broadcast_to([NP, 2 * BT, D // 2, 2]),
                                      kl[:, :, None, :].broadcast_to([NP, 2 * BT, D // 2, 2]), ALU.is_equal)
                    last = None
                    for out, key, n in ((m, key_m, NB * W), (r, key_r, RH * WG)):
                        last = dve.tensor_tensor(out.rearrange("p t (c two) -> p t c two", two=2),
                                                 iota_h[:, None, 0:n].rearrange("p o (c two) -> p o c two", two=2).broadcast_to([NP, BT, n // 2, 2]),
                                                 key[:, bass.ds(t0, BT), None, :].broadcast_to([NP, BT, n // 2, 2]), ALU.is_equal)
                    last.then_inc(ring_ready, 1)

        @block.gpsimd
        def _(pool):
            pool.memset(one_over, 1.0 / D).then_inc(put_a, 1)
            pool.memset(eps, EPS).then_inc(put_b, 1)
            pool.memset(power, -0.5).then_inc(powers, 1)
            pool.memset(zero, 0.0).then_inc(ring_free, 2)
            pool.memset(tmp[:, 0:1], 0.0).then_inc(parts_out, 16)
            pool.wait_ge(parts_out, 16)
            with pool.Fori(0, NB) as j:
                steps = [0]

                def link(ins):
                    steps[0] += 1
                    ins.then_inc(norm_step, 1)
                    pool.wait_ge(norm_step, j * 23 + steps[0])

                def total(out, v):
                    link(pool.tensor_tensor(tmp[:, 0:D // 2], v[:, 0:D // 2], v[:, D // 2:D], ALU.add))
                    n = D // 4
                    while n > 1:
                        link(pool.tensor_tensor(tmp[:, 0:n], tmp[:, 0:n], tmp[:, n:2 * n], ALU.add))
                        n //= 2
                    link(pool.tensor_tensor(out, tmp[:, 0:1], tmp[:, 1:2], ALU.add))

                def over(v):
                    return v.broadcast_to([NP, D])

                pool.wait_ge(x_loaded, j * 16 + 16)
                total(stat[:, 0:1], x_in)
                link(pool.tensor_tensor(stat[:, 0:1], stat[:, 0:1], one_over, ALU.mult))
                ins = pool.tensor_tensor(xc, x_in, over(stat[:, 0:1]), ALU.subtract)
                ins.then_inc(x_free, 1)
                pool.wait_ge(x_free, j + 1)
                link(pool.tensor_tensor(tmp, xc, xc, ALU.mult))
                total(stat[:, 1:2], tmp)
                ins = pool.tensor_tensor(stat[:, 1:2], stat[:, 1:2], one_over, ALU.mult)
                pool.tensor_scalar(xc, xc, 0.0, None, ALU.max).then_inc(norm_mid, 1)
                link(ins)
                link(pool.tensor_tensor(stat[:, 1:2], stat[:, 1:2], eps, ALU.add))
                link(pool.tensor_tensor(stat[:, 2:3], stat[:, 1:2], power, ALU.pow))
                pool.wait_ge(norm_mid, j * 2 + 1)
                link(pool.tensor_tensor(xc, xc, over(stat[:, 2:3]), ALU.mult))
                pool.wait_ge(parts_out, j * 16 + 16)
                link(pool.tensor_tensor(split[:, 0, :], xc, over(zero), ALU.add))
                link(pool.tensor_tensor(xc, xc, split[:, 0, :], ALU.subtract))
                link(pool.tensor_tensor(split[:, 1, :], xc, over(zero), ALU.add))
                pool.tensor_tensor(split[:, 2, :], xc, split[:, 1, :], ALU.subtract).then_inc(norm_mid, 1)

        @block.tensor
        def _(pe):
            regs = [[pe.alloc_register(f"place{g}_{k}") for k in range(1 + GT)] for g in range(4)]
            with pe.Fori(0, BATCHES // 2) as it:
                pe.reg_load([x for y in regs for x in y], places[0:1, bass.ds(it * 4 + 1, 4), :])
                for hb in range(2):
                    lo, m, r = ring[hb]
                    pe.wait_ge(ring_ready, it * 2 + (hb + 1))
                    for g in range(2):
                        a, b = banks[g]
                        win = [a[:, 0:HA * WG].rearrange("p (h d) -> p h d", d=WG),
                               b[:, 0:(HBK + RH) * WG].rearrange("p (h d) -> p h d", d=WG)]
                        grp = it * 4 + (hb * 2 + g + 1)
                        at0 = pe.snap(regs[hb * 2 + g][0], donate=True, min_val=0, max_val=N - WG)
                        shift = [pe.snap(x, donate=True, min_val=0, max_val=WG - W) for x in regs[hb * 2 + g][1:]]
                        for t in range(GT):
                            k = g * GT + t
                            d0 = shift[t]
                            s = t == 0
                            pe.matmul(win[0][:, :, bass.ds(d0, W)], lo[:, k, 0, :],
                                      m[:, k, 0:HA * W].rearrange("p (h d) -> p h d", d=W), start=s, stop=False, skip_group_check=True)
                            pe.matmul(win[1][:, 0:HBK, bass.ds(d0, W)], lo[:, k, 0, :],
                                      m[:, k, HA * W:].rearrange("p (h d) -> p h d", d=W), start=s, stop=False, skip_group_check=True)
                            last = pe.matmul(b[:, HBK * WG:(HBK + RH) * WG], lo[:, k, 1, :], r[:, k, :], start=False, stop=False, skip_group_check=True)
                        if g:
                            last.then_inc(ring_free, 1)
                        for w, put, done, h0, h1 in ((win[0], put_a, sum_a, 0, HA), (win[1], put_b, sum_b, HA, PL)):
                            pe.wait_ge(put, grp)
                            pe.matmul(w, ident_h[:, :], counts[:, h0:h1, bass.ds(at0, WG)], start=False, stop=True,
                                      skip_group_check=True).then_inc(done, 1)

        @block.scalar
        def _(act):
            regs = [act.alloc_register(f"start{g}") for g in range(8)]
            act.copy(table, one_row).then_inc(table_in, 1)
            with act.Fori(0, GROUPS // 8) as it:
                for g in range(8):
                    act.reg_load(regs[g], places[0:1, bass.ds(it * 8 + (g + 1), 1), 0:1])
                    at0 = act.snap(regs[g], donate=True, min_val=0, max_val=N - WG)
                    for p, n, put, done, h0, h1 in ((banks[g % 2][0], HA, put_a, sum_a, 0, HA), (banks[g % 2][1], HBK + RH, put_b, sum_b, HA, PL)):
                        act.wait_ge(done, it * 8 + (g + 1))
                        act.copy(counts[:, h0:h1, bass.ds(at0, WG)],
                                 p[:, 0:n * WG].rearrange("p (h d) -> p h d", d=WG)).then_inc(put, 1)
    local.close()


MOST = 2048


def check_counts(nc, ctx, T, src, dst, rel, parts_dram, rel_embed, w_r, w_sl, w_el):
    counts, work, small = T["counts"], T["work"], T["small"]

    def sem(name):
        return ctx.enter_context(nc.semaphore("c_" + name))

    P1 = places_of_layers(work)
    parts, rel_parts, wr, ws, rel_f, ones_h = (P1[k] for k in ("parts", "rel_parts", "wr", "ws", "rel_f", "ones_h"))
    norm, iso, some = small[:, 0, :], small[:, 1, :], small[:, 2, :]

    at = PARTS_B

    def place(rows, cols, dt, size):
        nonlocal at
        v = view(work, at, rows, cols, dt)
        at += cols * size
        assert at <= PARTS_B + HN_B
        return v

    node_i, dest_i, type_i = (place(NP, TILES, I32, 4) for _ in range(3))
    node, dest, kind = (v.bitcast(F32) for v in (node_i, dest_i, type_i))
    ramp_i = place(NP, NP, I32, 4)
    ramp = ramp_i.bitcast(F32)
    hot_l = place(NP, NP, F32, 4)
    hot_r = place(NP, NP, F32, 4)
    zeros = place(NP, NP, F32, 4)
    top, bad, one = place(NP, 1, F32, 4), place(NP, 1, F32, 4), place(NP, 1, F32, 4)

    local = ExitStack()
    ps_deg = local.enter_context(nc.psum_tensor("c_deg", [128, 512], F32))
    ps_bad = local.enter_context(nc.psum_tensor("c_bad", [128, 512], F32))
    ps_cnt = local.enter_context(nc.psum_tensor("c_cnt", [128, 512], F32))

    wts, parts_in, rel_step = T["wts1"], T["parts_in"], T["rel_step1"]
    ones_set, deg_done, deg_step, root_done, bad_ready, bad_sum, flagged = (
        sem(n) for n in ("ones_set", "deg_done", "deg_step", "root_done", "bad_ready", "bad_sum", "flagged"))
    edges_in, ramp_set, prep, hot, used, block_sum, block_out, again = (
        sem(n) for n in ("edges_in", "ramp_set", "prep", "hot", "used", "block_sum", "block_out", "again"))
    PLANES = ((0, NB, node, NP), (NB, PL, kind, RL))

    with nc.Block() as block:

        @block.sync
        def _(sp):
            for i in range(5):
                sp.dma_start(parts[:, 5 * i:5 * i + 5, :, :],
                             parts_dram.rearrange("(j p) (s f) -> p j s f", p=NP, s=3)[:, 5 * i:5 * i + 5, :, :]).then_inc(parts_in[i], 16)
            sp.dma_start(rel_f, rel_embed.rearrange("(h p) f -> p h f", p=RL)).then_inc(wts, 16)
            sp.dma_start(wr, w_r).then_inc(wts, 16)
            sp.dma_start(ws[:, 0:D], w_sl).then_inc(wts, 16)
            sp.dma_start(ws[:, D:], w_el).then_inc(wts, 16)
            sp.wait_ge(flagged, 1)
            flag = sp.alloc_register("again_sp")
            sp.reg_load(flag, T["flag"][0:1, 0:1])
            with sp.If_ne(flag, 0):
                with nc.allow_non_contiguous_dma("the second path loads the edges one by one"):
                    for t, v in ((node_i, src), (dest_i, dst), (type_i, rel)):
                        sp.dma_start(t, v.rearrange("(t p) -> p t", p=NP)).then_inc(edges_in, 16)

        @block.gpsimd
        def _(pool):
            pool.wait_ge(flagged, 1)
            flag = pool.alloc_register("again_pool")
            pool.reg_load(flag, T["flag"][0:1, 0:1])
            with pool.If_ne(flag, 0):
                pool.iota(ramp_i, pattern=[[1, NP]], base=0, channel_multiplier=0).then_inc(ramp_set, 1)

        def degrees(pe, done):
            for j in range(NB):
                for h in range(RH):
                    last = pe.matmul(ps_deg[0:NP, j:j + 1], counts[0:RL, NB + h, j * NP:(j + 1) * NP], ones_h, start=h == 0, stop=h == RH - 1)
            last.then_inc(done, 1)

        @block.tensor
        def _(pe):
            pe.wait_ge(ones_set, 2)
            degrees(pe, deg_done)
            pe.wait_ge(bad_ready, 1)
            pe.matmul(ps_bad[0:1, 0:1], bad, one, start=True, stop=True).then_inc(bad_sum, 1)
            pe.wait_ge(flagged, 1)
            flag = pe.alloc_register("again_pe")
            pe.reg_load(flag, T["flag"][0:1, 0:1])
            with pe.If_ne(flag, 0):
                pe.wait_ge(prep, 5)
                for p0, p1, keys, rows in PLANES:
                    with pe.Fori(p0, p1) as j:
                        with pe.Fori(0, NB) as c:
                            out = ps_cnt[0:rows, 0:NP]
                            pe.wait_ge(block_out, j * NB + c + 1)
                            pe.matmul(out, zeros[:, 0:rows], zeros, start=True, stop=False)
                            with pe.Fori(1, TILES + 1) as t:
                                pe.wait_ge(hot, (j * NB + c) * TILES + t)
                                pe.matmul(out, hot_l[:, 0:rows], hot_r, start=False, stop=False).then_inc(used, 1)
                            pe.matmul(out, zeros[:, 0:rows], zeros, start=False, stop=True).then_inc(block_sum, 1)
                pe.wait_ge(block_out, PL * NB + 1)
                degrees(pe, again)

        def norms(dve):
            dve.tensor_scalar(iso, ps_deg[0:NP, 0:NB], 0.0, None, ALU.is_equal).then_inc(deg_step, 1)
            dve.tensor_scalar(some, ps_deg[0:NP, 0:NB], 0.0, None, ALU.is_gt).then_inc(deg_step, 1)
            dve.tensor_scalar(norm, ps_deg[0:NP, 0:NB], 1.0, None, ALU.max).then_inc(deg_step, 1)

        @block.scalar
        def _(act):
            act.wait_ge(deg_step, 3)
            act.activation(norm, norm, ACT.Sqrt).then_inc(root_done, 1)
            act.wait_ge(flagged, 1)
            flag = act.alloc_register("again_act")
            act.reg_load(flag, T["flag"][0:1, 0:1])
            with act.If_ne(flag, 0):
                act.wait_ge(deg_step, 7)
                act.activation(norm, norm, ACT.Sqrt).then_inc(root_done, 1)

        @block.vector
        def _(dve):
            dve.memset(one, 1.0).then_inc(ones_set, 1)
            dve.memset(ones_h, 1.0).then_inc(ones_set, 1)
            dve.wait_ge(deg_done, 1)
            norms(dve)
            dve.tensor_reduce(top, ps_deg[0:NP, 0:NB], AX.X, ALU.max).then_inc(ones_set, 1)
            dve.wait_ge(ones_set, 3)
            dve.scalar_tensor_tensor(bad, top, float(MOST), T["outside"][:, :], ALU.is_ge, ALU.add).then_inc(bad_ready, 1)
            dve.wait_ge(root_done, 1)
            dve.reciprocal(norm, norm).then_inc(deg_step, 1)
            dve.wait_ge(bad_sum, 1)
            dve.tensor_scalar(T["flag"][:, :], ps_bad[0:1, 0:1], 0.0, None, ALU.is_gt).then_inc(flagged, 1)
            dve.wait_ge(wts, 16 * 4)
            for s in range(3):
                dve.tensor_copy(rel_parts[:, :, s, :], rel_f).then_inc(rel_step, 1)
                dve.wait_ge(rel_step, 2 * s + 1)
                dve.tensor_tensor(rel_f, rel_f, rel_parts[:, :, s, :], ALU.subtract).then_inc(rel_step, 1)
                dve.wait_ge(rel_step, 2 * s + 2)
            dve.wait_ge(flagged, 1)
            flag = dve.alloc_register("again_dve")
            dve.reg_load(flag, T["flag"][0:1, 0:1])
            with dve.If_ne(flag, 0):
                dve.wait_ge(edges_in, 48)
                dve.wait_ge(ramp_set, 1)
                for f, i in ((node, node_i), (dest, dest_i), (kind, type_i), (ramp, ramp_i)):
                    dve.tensor_copy(f, i).then_inc(prep, 1)
                dve.memset(zeros, 0.0).then_inc(prep, 1)
                dve.wait_ge(prep, 5)
                dve.tensor_copy(hot_l, zeros).then_inc(block_out, 1)
                dve.tensor_copy(hot_r, zeros).then_inc(used, 1)
                for p0, p1, keys, rows in PLANES:
                    with dve.Fori(p0, p1) as j:
                        with dve.Fori(0, NB) as c:
                            with dve.Fori(1, TILES + 1) as t:
                                dve.wait_ge(used, (j * NB + c) * TILES + t)
                                dve.tensor_tensor(hot_l, ramp, keys[:, bass.ds(t - 1, 1)].broadcast_to([NP, NP]), ALU.is_equal)
                                dve.tensor_tensor(hot_r, ramp, dest[:, bass.ds(t - 1, 1)].broadcast_to([NP, NP]), ALU.is_equal).then_inc(hot, 1)
                            dve.wait_ge(block_sum, j * NB + c + 1)
                            dve.tensor_copy(counts[0:rows, bass.ds(j, 1), bass.ds(c * NP, NP)].rearrange("p o d -> p (o d)"),
                                            ps_cnt[0:rows, 0:NP]).then_inc(block_out, 1)
                            dve.tensor_scalar(dest, dest, float(-NP), None, ALU.add).then_inc(again, 1)
                            dve.wait_ge(again, 2 * j + (j * NB + c) + 1)
                        dve.tensor_scalar(dest, dest, float(N), None, ALU.add).then_inc(again, 1)
                        dve.tensor_scalar(keys, keys, float(-rows), None, ALU.add).then_inc(again, 1)
                        dve.wait_ge(again, 2 * (j + 1) + (j + 1) * NB)
                dve.wait_ge(again, 2 * PL + PL * NB + 1)
                norms(dve)
                dve.wait_ge(root_done, 2)
                dve.reciprocal(norm, norm).then_inc(deg_step, 1)
    local.close()


def places_of_layers(work):
    at = 0
    found = {}

    def place(name, rows, cols, dt, size):
        nonlocal at
        found[name] = view(work, at, rows, cols, dt)
        at += cols * size
        assert at <= WORK

    place("parts", NP, NB * 3 * D, BF16, 2)
    place("hn", 128, NB * D, F32, 4)
    place("rel_parts", RL, RH * 3 * D, BF16, 2)
    place("wr", D, D, F32, 4)
    place("ws", D, 2 * D, F32, 4)
    found["end"] = at
    place("rel_f", RL, RH * D, F32, 4)
    place("ones_h", RL, 2, F16, 2)
    found["ones_h"] = found["ones_h"][:, 0:1]
    found["parts"] = found["parts"].rearrange("p (j s f) -> p j s f", s=3, f=D)
    found["rel_parts"] = found["rel_parts"].rearrange("p (h s f) -> p h s f", s=3, f=D)
    found["rel_f"] = found["rel_f"].rearrange("p (h f) -> p h f", f=D)
    return found


LB = 2
PARTS_B = NB * 3 * D * 2
HN_B = NB * D * 4


def message_layer(nc, ctx, T, layer, w_r, w_sl, w_el, aux):
    counts, work, small, ident, ident_h = T["counts"], T["work"], T["small"], T["ident"], T["ident_h"]
    last_layer = layer == 2
    L = f"l{layer}_"

    def sem(name):
        return ctx.enter_context(nc.semaphore(L + name))

    P1 = places_of_layers(work)
    parts, hn, rel_parts, wr, ws = (P1[k] for k in ("parts", "hn", "rel_parts", "wr", "ws"))
    hn_n = hn[0:NP, :].rearrange("p (j f) -> p j f", f=D)
    at = P1["end"]

    def place(rows, cols, dt, size):
        nonlocal at
        v = view(work, at, rows, cols, dt)
        at += cols * size
        assert at <= WORK
        return v

    agg_t = place(D, LB * NP, F32, 4)
    h_t = place(D, LB * NP, F32, 4)
    tmp = place(NP, LB * D, F32, 4).rearrange("p (b f) -> p b f", f=D)
    if last_layer:
        wqk = place(D, D, F32, 4)
        xc = place(NP, LB * D, F32, 4).rearrange("p (b f) -> p b f", f=D)
        h3_t = place(D, LB * NP, F32, 4)
        bqk = place(D, 1, F32, 4)
        bn = place(NP, LB * 6, F32, 4).rearrange("p (b k) -> p b k", k=6)
        mv = place(NP, LB * 2, F32, 4).rearrange("p (b k) -> p b k", k=2)
        rstd = place(NP, LB, F32, 4)
        mark = place(1, 1, F32, 4)
        power = place(NP, 1, F32, 4)
        power_set = sem("power_set")
        qk_t = hn
    norm, iso, some = small[:, 0, :], small[:, 1, :], small[:, 2, :]

    local = ExitStack()

    def ps(name, shape):
        return local.enter_context(nc.psum_tensor(L + name, shape, F32))

    ps_h, ps_g, ps_s, ps_a = ps("ps_h", [128, 512]), ps("ps_g", [128, 512]), ps("ps_s", [128, 512]), ps("ps_a", [128, 512])
    ps_x, ps_q = ps("ps_x", [128, 512]), ps("ps_q", [128, 512])
    self_v = ps_s[0:NP, :].rearrange("p (b k f) -> p b k f", b=LB, k=2)
    agg_v = ps_a[0:NP, 0:LB * D].rearrange("p (b f) -> p b f", f=D)

    parts_in = T["parts_in"]
    wts = sem("weights_in") if last_layer else T["wts1"]
    rounded, parts_ready = sem("rounded"), sem("parts_ready")
    turned, turned_out, summed, summed_out = sem("turned"), sem("turned_out"), sem("summed"), sem("summed_out")
    self_done, agg_done, el_out, step, chunk_done = sem("self_done"), sem("agg_done"), sem("el_out"), sem("step"), sem("chunk_done")
    x_in, x2_ready, x2_out, h3_ready, h3_out = sem("x_in"), sem("x2_ready"), sem("x2_out"), sem("h3_ready"), sem("h3_out")
    var_done, root_done, h3_turned, h3_t_out, qk_done, qk_out = (sem(n) for n in ("var_done", "root_done", "h3_turned", "h3_t_out", "qk_done", "qk_out"))
    FULL = NB // LB

    with nc.Block() as block:

        @block.sync
        def _(sp):
            if last_layer:
                sp.dma_start(wr, w_r).then_inc(wts, 16)
                sp.dma_start(ws[:, 0:D], w_sl).then_inc(wts, 16)
                sp.dma_start(ws[:, D:], w_el).then_inc(wts, 16)
                sp.dma_start(wqk, aux["wqk"]).then_inc(wts, 16)
                sp.dma_start(bqk, aux["bqk"].rearrange("(p o) -> p o", o=1)).then_inc(wts, 16)

                def chunk(c, nb):
                    known = isinstance(c, int)
                    at, before, this = (v if known else sp.snap(v) for v in (c * (LB * NP), c * 16, c + 1))
                    rows = lambda v: v[bass.ds(at, nb * NP), :].rearrange("(b p) f -> p b f", p=NP)
                    if not known or c > 0:
                        sp.wait_ge(h3_out, before)
                        sp.wait_ge(h3_turned, c)
                    sp.dma_start(xc[:, 0:nb, :], rows(aux["x"])).then_inc(x_in, 16)
                    sp.wait_ge(x2_ready, this)
                    sp.dma_start(rows(aux["x2"]), tmp[:, 0:nb, :]).then_inc(x2_out, 16)
                    sp.wait_ge(h3_ready, this)
                    sp.dma_start(rows(aux["h3"]), xc[:, 0:nb, :]).then_inc(h3_out, 16)

                chunk(0, LB)
                with sp.Fori(1, FULL) as c:
                    chunk(c, LB)
                chunk(FULL, NB - FULL * LB)
                sp.wait_ge(x2_out, 16 * (FULL + 1))
                sp.wait_ge(h3_out, 16 * (FULL + 1))

        @block.gpsimd
        def _(pool):
            if last_layer:
                def root(c, nb):
                    pool.wait_ge(var_done, c + 1)
                    pool.tensor_tensor(rstd[:, 0:nb], mv[:, 0:nb, 1], power.broadcast_to([NP, nb]), ALU.pow).then_inc(root_done, 1)

                pool.memset(power, -0.5).then_inc(power_set, 1)
                pool.wait_ge(power_set, 1)
                root(0, LB)
                with pool.Fori(1, FULL) as c:
                    root(c, LB)
                root(FULL, NB - FULL * LB)

        @block.tensor
        def _(pe):
            def own(c, nb):
                for b in range(nb):
                    for s in range(3):
                        if isinstance(c, int):
                            lhs = parts[:, c * LB + b, s, :]
                        else:
                            lhs = parts[:, bass.ds(c * LB + b, 1), s, :].rearrange("p o f -> p (o f)")
                        last = pe.matmul(ps_h[:, b * NP:(b + 1) * NP], lhs, ident_h[0:NP, 0:NP], start=s == 0, stop=s == 2)
                last.then_inc(turned, 1)

            def sums(c, nb, first=False):
                cols = bass.ds(c * (LB * NP), nb * NP)
                for j in range(NB):
                    if first and j % 5 == 0:
                        (pe.wait_ge(parts_ready, 2 * (j // 5) + 2) if last_layer else pe.wait_ge(parts_in[j // 5], 16))
                    for s in range(3):
                        pe.matmul(ps_g[:, 0:nb * NP], parts[:, j, s, :], counts[0:NP, j, cols], start=j == 0 and s == 0, stop=False)
                for h in range(RH):
                    for s in range(3):
                        last = pe.matmul(ps_g[:, 0:nb * NP], rel_parts[:, h, s, :], counts[0:RL, NB + h, cols], start=False, stop=h == RH - 1 and s == 2)
                last.then_inc(summed, 1)

            def h3_turn(c, nb):
                pe.wait_ge(h3_ready, c + 1)
                for b in range(nb):
                    last = pe.transpose(ps_x[:, b * NP:(b + 1) * NP], xc[:, b, :], ident[0:NP, 0:NP])
                last.then_inc(h3_turned, 1)

            def weigh(c, nb, first=False):
                if first:
                    pe.wait_ge(wts, 16 * (5 if last_layer else 4))
                pe.wait_ge(turned_out, c + 1)
                if not first:
                    pe.wait_ge(chunk_done, c)
                for b in range(nb):
                    last = pe.matmul(self_v[:, b, :, :].rearrange("p k f -> p (k f)"), h_t[:, b * NP:(b + 1) * NP], ws, start=True, stop=True)
                last.then_inc(self_done, 1)
                pe.wait_ge(summed_out, c + 1)
                for b in range(nb):
                    last = pe.matmul(agg_v[:, b, :], agg_t[:, b * NP:(b + 1) * NP], wr, start=True, stop=True)
                last.then_inc(agg_done, 1)

            def qk(c, nb):
                pe.wait_ge(h3_t_out, c + 1)
                pe.matmul(ps_q[:, 0:nb * NP], wqk, h3_t[:, 0:nb * NP], start=True, stop=True).then_inc(qk_done, 1)

            if last_layer:
                pe.wait_ge(parts_ready, 2)
            else:
                pe.wait_ge(parts_in[0], 16)
            own(0, LB)
            sums(0, LB, True)
            weigh(0, LB, True)
            with pe.Fori(1, FULL) as c:
                own(c, LB)
                sums(c, LB)
                if last_layer:
                    h3_turn(c - 1, LB)
                weigh(c, LB)
                if last_layer:
                    qk(c - 1, LB)
            own(FULL, NB - FULL * LB)
            sums(FULL, NB - FULL * LB)
            if last_layer:
                h3_turn(FULL - 1, LB)
            weigh(FULL, NB - FULL * LB)
            if last_layer:
                qk(FULL - 1, LB)
                h3_turn(FULL, NB - FULL * LB)
                qk(FULL, NB - FULL * LB)

        @block.scalar
        def _(act):
            if last_layer:
                for i in range(5):
                    v = slice(5 * i, 5 * i + 5)
                    act.copy(parts[:, v, 0, :], hn_n[:, v, :]).then_inc(rounded, 1)
                    act.wait_ge(parts_ready, 2 * i + 1)
                    act.copy(parts[:, v, 1, :], hn_n[:, v, :]).then_inc(rounded, 1)

            def chunk(c, nb):
                act.wait_ge(turned, c + 1)
                act.copy(h_t[:, 0:nb * NP], ps_h[:, 0:nb * NP]).then_inc(turned_out, 1)
                act.wait_ge(summed, c + 1)
                act.copy(agg_t[:, 0:nb * NP], ps_g[:, 0:nb * NP]).then_inc(summed_out, 1)
                if last_layer and not (isinstance(c, int) and c == 0):
                    late(c - 1, LB)
                act.wait_ge(self_done, c + 1)
                for b in range(nb):
                    at = (c * LB + b)
                    act.mul(tmp[:, b, :], self_v[:, b, 1, :], iso[:, bass.ds(at, 1)]).then_inc(el_out, 1)

            def late(c, nb):
                act.wait_ge(h3_turned, c + 1)
                act.copy(h3_t[:, 0:nb * NP], ps_x[:, 0:nb * NP]).then_inc(h3_t_out, 1)

            def rows(c, nb):
                act.wait_ge(qk_done, c + 1)
                act.activation(qk_t[:, bass.ds(c * (LB * NP), nb * NP)], ps_q[:, 0:nb * NP], ACT.Identity, bias=bqk).then_inc(qk_out, 1)

            if last_layer:
                act.wait_ge(wts, 16 * 5)
            chunk(0, LB)
            with act.Fori(1, FULL) as c:
                chunk(c, LB)
                if last_layer:
                    rows(c - 1, LB)
            chunk(FULL, NB - FULL * LB)
            if last_layer:
                rows(FULL - 1, LB)
                late(FULL, NB - FULL * LB)
                rows(FULL, NB - FULL * LB)

        @block.vector
        def _(dve):
            if last_layer:
                for i in range(5):
                    v = slice(5 * i, 5 * i + 5)
                    dve.wait_ge(rounded, 2 * i + 1)
                    dve.tensor_tensor(hn_n[:, v, :], hn_n[:, v, :], parts[:, v, 0, :], ALU.subtract).then_inc(parts_ready, 1)
                    dve.wait_ge(rounded, 2 * i + 2)
                    dve.tensor_tensor(parts[:, v, 2, :], hn_n[:, v, :], parts[:, v, 1, :], ALU.subtract).then_inc(parts_ready, 1)

            def chunk(c, nb, per):
                done = [0]

                def link(ins):
                    done[0] += 1
                    ins.then_inc(step, 1)
                    dve.wait_ge(step, c * per + done[0])

                dve.wait_ge(el_out, c * LB + nb)
                for b in range(nb):
                    dve.scalar_tensor_tensor(tmp[:, b, :], self_v[:, b, 0, :], some[:, bass.ds(c * LB + b, 1)], tmp[:, b, :], ALU.mult, ALU.add)\
                       .then_inc(step, 1)
                    done[0] += 1
                dve.wait_ge(agg_done, c + 1)
                dve.wait_ge(step, c * per + done[0])
                for b in range(nb):
                    ins = dve.scalar_tensor_tensor(tmp[:, b, :], agg_v[:, b, :], norm[:, bass.ds(c * LB + b, 1)], tmp[:, b, :], ALU.mult, ALU.add)
                    done[0] += 1
                    ins.then_inc(step, 1)
                dve.wait_ge(step, c * per + done[0])
                t = tmp[:, 0:nb, :]
                if not last_layer:
                    dve.scalar_tensor_tensor(hn_n[:, bass.ds(c * LB, nb), :], t, SLOPE, t, ALU.mult, ALU.max).then_inc(chunk_done, 1)
                    return
                xv = xc[:, 0:nb, :]
                link(dve.scalar_tensor_tensor(t, t, SLOPE, t, ALU.mult, ALU.max))
                dve.wait_ge(x_in, c * 16 + 16)
                dve.tensor_tensor(t, t, xv, ALU.add).then_inc(x2_ready, 1)
                dve.wait_ge(x2_ready, c + 1)
                for b in range(nb):
                    ins = dve.bn_stats(bn[:, b, :], tmp[:, b, :])
                    done[0] += 1
                    ins.then_inc(step, 1)
                dve.wait_ge(step, c * per + done[0])
                dve.tensor_copy(mark, bn[0:1, 0, 0:1])
                for b in range(nb):
                    ins = dve.bn_aggr(mv[:, b, :], bn[:, b, :])
                    done[0] += 1
                    ins.then_inc(step, 1)
                dve.wait_ge(step, c * per + done[0])
                dve.tensor_scalar(mv[:, 0:nb, 1], mv[:, 0:nb, 1], EPS, None, ALU.add).then_inc(var_done, 1)
                dve.wait_ge(root_done, c + 1)
                for b in range(nb):
                    link(dve.tensor_scalar(xc[:, b, :], tmp[:, b, :], mv[:, b, 0:1], rstd[:, b:b + 1], ALU.subtract, ALU.mult))
                dve.tensor_scalar(xv, xv, 0.0, None, ALU.max).then_inc(h3_ready, 1)
                dve.wait_ge(x2_out, c * 16 + 16)
                dve.memset(rstd[0:1, 0:1], 1.0).then_inc(chunk_done, 1)

            per = 2 * LB + (1 + 3 * LB if last_layer else 0)
            chunk(0, LB, per)
            with dve.Fori(1, FULL) as c:
                chunk(c, LB, per)
            chunk(FULL, NB - FULL * LB, per)
    local.close()


AB = 4
CLIP = 5.0


def attention(nc, ctx, T, wv, bv, wo, bo, gamma, beta, x2, h3d, out):
    counts, work, small = T["counts"], T["work"], T["small"]

    def sem(name):
        return ctx.enter_context(nc.semaphore("a_" + name))

    at = 0

    def place(rows, cols):
        nonlocal at
        v = view(work, at, rows, cols, F32)
        at += cols * 4
        assert at <= WORK
        return v

    WIDE = AB * NP
    h3 = place(NP, NB * D).rearrange("p (j f) -> p j f", f=D)
    pbuf = [place(NP, WIDE) for _ in range(3)]
    ones, zero, power = place(NP, 1), place(NP, 1), place(NP, 1)
    bv_c = place(D, 1)
    inv = place(NP, AB)
    bn = place(NP, 2 * 6).rearrange("p (b k) -> p b k", k=6)
    mv = place(NP, 2 * 2).rearrange("p (b k) -> p b k", k=2)
    rstd = place(NP, 2)
    mark = place(1, 1)
    assert at <= PARTS_B
    at = PARTS_B
    qk_t = place(D, N)
    acc = place(NP, WIDE)
    hv = place(D, WIDE)
    y = place(NP, 2 * D).rearrange("p (b f) -> p b f", f=D)
    xr = place(NP, 2 * D).rearrange("p (b f) -> p b f", f=D)
    bo_b, gamma_b, beta_b, bvo = (place(NP, D) for _ in range(4))
    wv_s, wo_s = place(D, D), place(D, D)
    some = small[:, 2, :]

    local = ExitStack()

    def ps(name):
        return local.enter_context(nc.psum_tensor("a_" + name, [128, 512], F32))

    ps_s = [ps(f"ps_s{i}") for i in range(4)]
    ps_o, ps_v, ps_f, ps_n = ps("ps_o"), ps("ps_v"), ps("ps_f"), ps("ps_n")
    scores, clipped, exped, p_ready, pv_done, acc_done = (sem(n) for n in ("scores", "clipped", "exped", "p_ready", "pv_done", "acc_done"))
    loaded, h3_in, ones_set, bvb, bvo_done, bvo_out = (sem(n) for n in ("loaded", "h3_in", "ones_set", "bvb", "bvo_done", "bvo_out"))
    n_done, hv_out, v_done, v_out, f_done, inv_step, step = (sem(n) for n in ("n_done", "hv_out", "v_done", "v_out", "f_done", "inv_step", "step"))
    zero_set = sem("zero_set")
    var_done, root_done, xr_in, y_ready, y_out = (sem(n) for n in ("var_done", "root_done", "xr_in", "y_ready", "y_out"))
    FULL = NB // AB
    UNITS = (NB + AB - 1) // AB
    assert NB - FULL * AB == 1
    FIRST = (4, 15)

    def bc(v):
        return v.rearrange("(o f) -> o f", o=1).broadcast_to([NP, D])

    def pairs(nb):
        return [(h, min(2, nb - 2 * h)) for h in range((nb + 1) // 2)]

    with nc.Block() as block:

        @block.sync
        def _(sp):
            sp.dma_start(h3, h3d.rearrange("(j p) f -> p j f", p=NP)).then_inc(h3_in, 16)
            for s, v in ((wv_s, wv), (wo_s, wo), (bv_c, bv.rearrange("(p o) -> p o", o=1)), (bo_b, bc(bo)), (gamma_b, bc(gamma)), (beta_b, bc(beta))):
                sp.dma_start(s, v).then_inc(loaded, 16)

            def ends(c, nb):
                for h, n in pairs(nb):
                    known = isinstance(c, int)
                    at, q, this = (v if known else sp.snap(v) for v in (c * WIDE + 2 * h * NP, c * 2 + h, c * 2 + (h + 1)))
                    rows = lambda v: v[bass.ds(at, n * NP), :].rearrange("(b p) f -> p b f", p=NP)
                    if not (known and q == 0):
                        sp.wait_ge(y_ready, q)
                    sp.dma_start(xr[:, 0:n, :], rows(x2)).then_inc(xr_in, 16)
                    sp.wait_ge(y_ready, this)
                    sp.dma_start(rows(out), y[:, 0:n, :]).then_inc(y_out, 16)

            ends(0, AB)
            with sp.Fori(1, FULL) as c:
                ends(c, AB)
            ends(FULL, NB - FULL * AB)
            sp.wait_ge(y_out, 16 * (2 * FULL + 1))

        @block.tensor
        def _(pe):
            def score(c, nb, j):
                last = pe.matmul(ps_s[j % 4][0:NP, 0:nb * NP], qk_t[:, j * NP:(j + 1) * NP], qk_t[:, bass.ds(c * WIDE, nb * NP)],
                                 start=True, stop=True)
                last.then_inc(scores, 1)

            def chunk(c, nb, prev):
                for j in range(3):
                    score(c, nb, j)
                if not prev:
                    pe.wait_ge(h3_in, 16)
                if prev:
                    pe.wait_ge(acc_done, c * NB)
                    for b in range(prev):
                        last = pe.matmul(ps_n[0:NP, b:b + 1], acc[:, b * NP:(b + 1) * NP], ones, start=True, stop=True)
                    last.then_inc(n_done, 1)
                    pe.wait_ge(hv_out, c)
                for j in range(NB):
                    if j + 3 < NB:
                        score(c, nb, j + 3)
                    pe.wait_ge(p_ready, c * NB + (j + 1))
                    pe.matmul(ps_o[:, 0:nb * NP], h3[:, j, :], pbuf[j % 3][:, 0:nb * NP], start=j == 0, stop=j == NB - 1).then_inc(pv_done, 1)
                    if prev and j == 1:
                        project(c - 1, prev)
                    if prev and j == 3:
                        final(c - 1, prev)
                    if not prev and j == 6:
                        pe.wait_ge(bvb, 1)
                        pe.matmul(ps_f[0:NP, 0:D], hv[:, 0:NP], wo_s, start=True, stop=True).then_inc(bvo_done, 1)

            def project(c, nb):
                pe.wait_ge(hv_out, c + 1)
                pe.matmul(ps_v[:, 0:nb * NP], wv_s, hv[:, 0:nb * NP], start=True, stop=True).then_inc(v_done, 1)

            def final(c, nb):
                pe.wait_ge(v_out, c + 1)
                for b in range(nb):
                    last = pe.matmul(ps_f[0:NP, b * D:(b + 1) * D], hv[:, b * NP:(b + 1) * NP], wo_s, start=True, stop=True)
                last.then_inc(f_done, 1)

            chunk(0, AB, 0)
            with pe.Fori(1, FULL) as c:
                chunk(c, AB, AB)
            def wide_scores(u):
                js = range(u * AB, min(u * AB + AB, NB))
                for i, j in enumerate(js):
                    last = pe.matmul(ps_s[u % 4][0:NP, i * NP:(i + 1) * NP], qk_t[:, j * NP:(j + 1) * NP], qk_t[:, FULL * WIDE:], start=True, stop=True)
                last.then_inc(scores, 1)

            for u in range(3):
                wide_scores(u)
            pe.wait_ge(acc_done, FULL * NB)
            for b in range(AB):
                last = pe.matmul(ps_n[0:NP, b:b + 1], acc[:, b * NP:(b + 1) * NP], ones, start=True, stop=True)
            last.then_inc(n_done, 1)
            pe.wait_ge(hv_out, FULL)
            for u in range(UNITS):
                if u + 3 < UNITS:
                    wide_scores(u + 3)
                pe.wait_ge(p_ready, FULL * NB + u + 1)
                js = range(u * AB, min(u * AB + AB, NB))
                for i, j in enumerate(js):
                    last = pe.matmul(ps_o[:, 0:NP], h3[:, j, :], pbuf[u % 3][:, i * NP:(i + 1) * NP], start=j == 0, stop=j == NB - 1)
                last.then_inc(pv_done, 1)
                if u == 1:
                    project(FULL - 1, AB)
                if u == 3:
                    final(FULL - 1, AB)
            pe.wait_ge(acc_done, FULL * NB + UNITS)
            pe.wait_ge(inv_step, 2 * FULL - 1)
            for b in range(AB):
                last = pe.matmul(ps_n[0:NP, 0:1], acc[:, b * NP:(b + 1) * NP], ones, start=b == 0, stop=b == AB - 1)
            last.then_inc(n_done, 1)
            project(FULL, 1)
            pe.wait_ge(y_ready, 2 * FULL)
            final(FULL, 1)

        @block.gpsimd
        def _(pool):
            def root(c, h, n):
                pool.wait_ge(var_done, c * 2 + (h + 1))
                pool.tensor_tensor(rstd[:, 0:n], mv[:, 0:n, 1], power.broadcast_to([NP, n]), ALU.pow).then_inc(root_done, 1)

            def chunk(c, nb, prev):
                for j in range(NB):
                    for h, n in pairs(prev):
                        if j == FIRST[h] + 5:
                            root(c - 1, h, n)
                    pool.wait_ge(p_ready, c * NB + (j + 1))
                    p = pbuf[j % 3][:, 0:nb * NP]
                    a = acc[:, 0:nb * NP]
                    if j == 0:
                        if not isinstance(c, int) or c > 0:
                            pool.wait_ge(n_done, c)
                        pool.tensor_tensor(a, p, zero.broadcast_to([NP, nb * NP]), ALU.add).then_inc(acc_done, 1)
                    else:
                        pool.wait_ge(acc_done, c * NB + j)
                        pool.tensor_tensor(a, a, p, ALU.add).then_inc(acc_done, 1)

            pool.memset(zero, 0.0).then_inc(zero_set, 1)
            pool.memset(power, -0.5).then_inc(zero_set, 1)
            pool.wait_ge(zero_set, 2)
            chunk(0, AB, 0)
            with pool.Fori(1, FULL) as c:
                chunk(c, AB, AB)
            for u in range(UNITS):
                n = min(AB, NB - u * AB) * NP
                pool.wait_ge(p_ready, FULL * NB + u + 1)
                if u == 0:
                    pool.wait_ge(n_done, FULL)
                    pool.tensor_tensor(acc, pbuf[0], zero.broadcast_to([NP, WIDE]), ALU.add).then_inc(acc_done, 1)
                else:
                    pool.wait_ge(acc_done, FULL * NB + u)
                    pool.tensor_tensor(acc[:, 0:n], acc[:, 0:n], pbuf[u % 3][:, 0:n], ALU.add).then_inc(acc_done, 1)
                if u == UNITS - 2:
                    root(FULL - 1, 0, 2)
            root(FULL - 1, 1, 2)
            root(FULL, 0, 1)

        @block.scalar
        def _(act):
            def take(c, nb):
                act.wait_ge(pv_done, (c + 1) * NB)
                act.copy(hv[:, 0:nb * NP], ps_o[:, 0:nb * NP]).then_inc(hv_out, 1)

            def projected(c, nb):
                act.wait_ge(v_done, c + 1)
                act.copy(hv[:, 0:nb * NP], ps_v[:, 0:nb * NP]).then_inc(v_out, 1)

            def chunk(c, nb, prev):
                for j in range(NB):
                    act.wait_ge(clipped, c * NB + (j + 1))
                    s = ps_s[j % 4][0:NP, 0:nb * NP]
                    act.activation(s, s, ACT.Exp, scale=float(D) ** -0.5).then_inc(exped, 1)
                    if prev:
                        if j == 0:
                            take(c - 1, prev)
                        if j == 2:
                            projected(c - 1, prev)
                    elif j == 8:
                        act.wait_ge(bvo_done, 1)
                        act.copy(bvo, ps_f[0:NP, 0:D]).then_inc(bvo_out, 1)

            chunk(0, AB, 0)
            with act.Fori(1, FULL) as c:
                chunk(c, AB, AB)
            for u in range(UNITS):
                act.wait_ge(clipped, FULL * NB + u + 1)
                s = ps_s[u % 4][0:NP, 0:min(AB, NB - u * AB) * NP]
                act.activation(s, s, ACT.Exp, scale=float(D) ** -0.5).then_inc(exped, 1)
                if u == 0:
                    take(FULL - 1, AB)
                if u == 2:
                    projected(FULL - 1, AB)
            act.wait_ge(pv_done, FULL * NB + UNITS)
            act.copy(hv[:, 0:NP], ps_o[:, 0:NP]).then_inc(hv_out, 1)
            projected(FULL, 1)

        @block.vector
        def _(dve):
            COUNTS = (2, 2, 1, 2, 2, 2, 1, 1)
            PER = sum(COUNTS)

            def clip(c, nb, j):
                dve.wait_ge(scores, c * NB + (j + 1))
                s = ps_s[j % 4][0:NP, 0:nb * NP]
                dve.tensor_scalar(s, s, CLIP * float(D) ** 0.5, -CLIP * float(D) ** 0.5, ALU.min, ALU.max).then_inc(clipped, 1)

            def weigh(c, nb, j):
                dve.wait_ge(exped, c * NB + (j + 1))
                if not (isinstance(c, int) and c == 0 and j < 3):
                    dve.wait_ge(pv_done, c * NB + (j - 2 if j else 0))
                    dve.wait_ge(acc_done, c * NB + (j - 2 if j else 0))
                dve.tensor_tensor(pbuf[j % 3][:, 0:nb * NP], ps_s[j % 4][0:NP, 0:nb * NP], counts[0:NP, j, bass.ds(c * WIDE, nb * NP)],
                                  ALU.mult).then_inc(p_ready, 1)

            def begin(c, nb):
                dve.wait_ge(n_done, c + 1)
                dve.tensor_scalar(inv[:, 0:nb], ps_n[0:NP, 0:nb], 1e-30, None, ALU.max).then_inc(inv_step, 1)
                dve.wait_ge(inv_step, c * 2 + 1)
                dve.reciprocal(inv[:, 0:nb], inv[:, 0:nb]).then_inc(inv_step, 1)
                dve.wait_ge(inv_step, c * 2 + 2)
                dve.wait_ge(f_done, c + 1)

            def ending(c, h, n, part):
                q = c * 2 + h
                at = c * AB + 2 * h
                v = y[:, 0:n, :]

                def parts_done():
                    dve.wait_ge(step, q * PER + sum(n if k == 2 else 1 for k in COUNTS[:part]))

                if part == 0:
                    if not (isinstance(c, int) and c == 0 and h == 0):
                        dve.wait_ge(y_out, q * 16)
                    for b in range(n):
                        dve.scalar_tensor_tensor(y[:, b, :], ps_f[0:NP, (2 * h + b) * D:(2 * h + b + 1) * D], inv[:, 2 * h + b:2 * h + b + 1],
                                                 h3[:, bass.ds(at + b, 1), :].rearrange("p o f -> p (o f)"), ALU.mult, ALU.add).then_inc(step, 1)
                if part == 1:
                    parts_done()
                    for b in range(n):
                        dve.scalar_tensor_tensor(y[:, b, :], bvo, some[:, bass.ds(at + b, 1)], y[:, b, :], ALU.mult, ALU.add).then_inc(step, 1)
                if part == 2:
                    parts_done()
                    dve.tensor_tensor(v, v, bo_b[:, None, :].broadcast_to([NP, n, D]), ALU.add).then_inc(step, 1)
                if part == 3:
                    parts_done()
                    for b in range(n):
                        dve.bn_stats(bn[:, b, :], y[:, b, :]).then_inc(step, 1)
                if part == 4:
                    parts_done()
                    dve.tensor_copy(mark, bn[0:1, 0, 0:1])
                    for b in range(n):
                        dve.bn_aggr(mv[:, b, :], bn[:, b, :]).then_inc(step, 1)
                    dve.wait_ge(step, q * PER + sum(n if k == 2 else 1 for k in COUNTS[:part + 1]))
                    dve.tensor_scalar(mv[:, 0:n, 1], mv[:, 0:n, 1], EPS, None, ALU.add).then_inc(var_done, 1)
                if part == 5:
                    dve.wait_ge(root_done, q + 1)
                    for b in range(n):
                        dve.tensor_scalar(y[:, b, :], y[:, b, :], mv[:, b, 0:1], rstd[:, b:b + 1], ALU.subtract, ALU.mult).then_inc(step, 1)
                if part == 6:
                    parts_done()
                    dve.tensor_tensor(v, v, gamma_b[:, None, :].broadcast_to([NP, n, D]), ALU.mult).then_inc(step, 1)
                if part == 7:
                    parts_done()
                    dve.tensor_tensor(v, v, beta_b[:, None, :].broadcast_to([NP, n, D]), ALU.add).then_inc(step, 1)
                if part == 8:
                    parts_done()
                    dve.wait_ge(xr_in, q * 16 + 16)
                    dve.tensor_tensor(v, v, xr[:, 0:n, :], ALU.add).then_inc(y_ready, 1)

            def chunk(c, nb, prev):
                clip(c, nb, 0)
                clip(c, nb, 1)
                for j in range(NB):
                    if j + 2 < NB:
                        clip(c, nb, j + 2)
                    weigh(c, nb, j)
                    if prev:
                        if j == FIRST[0]:
                            begin(c - 1, prev)
                        for h, n in pairs(prev):
                            if FIRST[h] <= j < FIRST[h] + 5:
                                ending(c - 1, h, n, j - FIRST[h])
                            if FIRST[h] + 6 <= j < FIRST[h] + 10:
                                ending(c - 1, h, n, j - FIRST[h] - 1)
                    elif j == 4:
                        dve.wait_ge(loaded, 16 * 6)
                        dve.tensor_copy(hv[:, 0:NP], bv_c.broadcast_to([D, NP])).then_inc(bvb, 1)
                    elif j == 10:
                        dve.wait_ge(bvo_out, 1)

            dve.memset(ones, 1.0).then_inc(ones_set, 1)
            chunk(0, AB, 0)
            with dve.Fori(1, FULL) as c:
                chunk(c, AB, AB)
            def wide_clip(u):
                dve.wait_ge(scores, FULL * NB + u + 1)
                s = ps_s[u % 4][0:NP, 0:min(AB, NB - u * AB) * NP]
                dve.tensor_scalar(s, s, CLIP * float(D) ** 0.5, -CLIP * float(D) ** 0.5, ALU.min, ALU.max).then_inc(clipped, 1)

            wide_clip(0)
            wide_clip(1)
            for u in range(UNITS):
                if u + 2 < UNITS:
                    wide_clip(u + 2)
                n = min(AB, NB - u * AB)
                before = FULL * NB + max(u - 2, 0)
                dve.wait_ge(exped, FULL * NB + u + 1)
                dve.wait_ge(pv_done, before)
                dve.wait_ge(acc_done, before)
                dve.tensor_tensor(pbuf[u % 3][:, 0:n * NP].rearrange("p (j d) -> p j d", d=NP),
                                  ps_s[u % 4][0:NP, 0:n * NP].rearrange("p (j d) -> p j d", d=NP),
                                  counts[0:NP, u * AB:u * AB + n, FULL * WIDE:], ALU.mult).then_inc(p_ready, 1)
                if u == UNITS - 3:
                    begin(FULL - 1, AB)
                    for part in range(5):
                        ending(FULL - 1, 0, 2, part)
            for part in range(5, 9):
                ending(FULL - 1, 0, 2, part)
            for part in range(9):
                ending(FULL - 1, 1, 2, part)
            begin(FULL, 1)
            for part in range(9):
                ending(FULL, 0, 1, part)
    local.close()


def program(nc, x, src, dst, rel, rel_embed, w_r1, w_sl1, w_el1, w_r2, w_sl2, w_el2, wqk, bqk, wv, bv, wo, bo, gamma, beta, out):
    parts_dram = nc.dram_tensor("h_parts", (N, 3 * D), BF16).ap()
    x2 = nc.dram_tensor("x_after_messages", (N, D), F32).ap()
    h3 = nc.dram_tensor("h_attention", (N, D), F32).ap()
    with ExitStack() as ctx:
        def sb(name, shape, dt):
            return ctx.enter_context(nc.sbuf_tensor(name, shape, dt))

        flat = sb("counts", [128, PL * N + PL * N % 2], F16)
        T = {"counts_flat": flat, "counts": flat[:, 0:PL * N].rearrange("p (h d) -> p h d", d=N),
             "work": sb("work", [128, WORK // 4], F32), "ident": sb("ident", [128, 128], F32),
             "ident_h": sb("ident_h", [128, 128], F16), "small": sb("small", [NP, 3, NB], F32), "outside": sb("outside", [NP, 1], F32),
             "flag": sb("flag", [1, 1], I32)}
        build_counts(nc, ctx, T, src, dst, rel, x, parts_dram)
        T["wts1"] = ctx.enter_context(nc.semaphore("weights1_in"))
        T["rel_step1"] = ctx.enter_context(nc.semaphore("rel_step"))
        T["parts_in"] = [ctx.enter_context(nc.semaphore(f"parts_in{i}")) for i in range(5)]
        check_counts(nc, ctx, T, src, dst, rel, parts_dram, rel_embed, w_r1, w_sl1, w_el1)
        message_layer(nc, ctx, T, 1, None, None, None, {})
        message_layer(nc, ctx, T, 2, w_r2, w_sl2, w_el2, {"x": x, "x2": x2, "h3": h3, "wqk": wqk, "bqk": bqk})
        attention(nc, ctx, T, wv, bv, wo, bo, gamma, beta, x2, h3, out)


_INS = ["x", "src", "dst", "edge_type_200", "L0_gnn_rel_embed", "L0_gnn_W_r1", "L0_gnn_W_sl1", "L0_gnn_W_el1", "L0_gnn_W_r2", "L0_gnn_W_sl2",
        "L0_gnn_W_el2", "L1_gnn_Wqk", "L1_gnn_bqk", "L1_gnn_Wv", "L1_gnn_bv", "L1_gnn_Wo", "L1_gnn_bo", "L1_gnn_gamma", "L1_gnn_beta"]


def kernel(**inputs):
    import concourse.bacc as bacc
    from concourse.bass_utils import run_bass_kernel_spmd

    nc = bacc.Bacc("TRN2", target_bir_lowering=False, num_devices=1)
    arrays, args = {}, []
    for name in _INS:
        a = np.ascontiguousarray(inputs[name])
        arrays[f"in_{name}"] = a
        args.append(nc.dram_tensor(f"in_{name}", a.shape, mybir.dt.from_np(a.dtype), kind="ExternalInput").ap())
    args.append(nc.dram_tensor("out_0", (N, D), F32, kind="ExternalOutput").ap())
    program(nc, *args)
    r = run_bass_kernel_spmd(nc, [arrays], core_ids=[0])
    return r.results[0]["out_0"]
```
